# Optimizing a Trainium2 kernel written in Bass

```python
import numpy as np
import jax
import jax.numpy as jnp

def _softmax(x, axis=-1):
    return jax.nn.softmax(x, axis=axis)

def _gelu(x):
    return jax.nn.gelu(x, approximate=True)

def _silu(x):
    return jax.nn.silu(x)

def _sigmoid(x):
    return jax.nn.sigmoid(x)

def _layernorm(x, axis=-1, eps=1e-05):
    m = jnp.mean(x, axis=axis, keepdims=True)
    v = jnp.var(x, axis=axis, keepdims=True)
    return (x - m) / jnp.sqrt(v + eps)

def _scatter_add(tgt, idx, src, axis=0):
    return tgt.at[idx].add(src)

def _segment_sum(src, seg, n):
    return jax.ops.segment_sum(src, seg, n)
kernel_name = 'mk_flamingo_gated_d1_seqx_r4_462b58'

def setup_inputs(seed: int=0):
    np.random.seed(seed)
    _w = jnp.asarray

    def _rec_inputs():
        import jax
        import jax.numpy as jnp
        _rk = jax.random.key(seed)
        x = 7.22e-05 + 1 * jax.random.normal(jax.random.fold_in(_rk, 1), (16, 128, 512), jnp.float32)
        _lenS = 128 - jax.random.randint(jax.random.fold_in(_rk, 7), (16,), 0, max(1, 128 // 4) + 1, jnp.int32)
        _lenS2 = 128 - jax.random.randint(jax.random.fold_in(_rk, 8), (16,), 0, max(1, 128 // 4) + 1, jnp.int32)
        _ctx_512P = jax.random.normal(jax.random.fold_in(_rk, 11), (16, 16, 128), jnp.float32)
        _ctx_512c = jax.random.dirichlet(jax.random.fold_in(_rk, 511), 0.3 * jnp.ones((16,), jnp.float32), (16, 128))
        _ctx_512t = jnp.einsum('bsk,bkd->bsd', _ctx_512c, _ctx_512P)
        _ctx_512t = _ctx_512t * jax.lax.rsqrt(jnp.mean(jnp.square(_ctx_512t)) + 1e-12) * 0.953939
        ctx_512 = -0.000514642 + 1.00011 * (_ctx_512t + 0.3 * jax.random.normal(jax.random.fold_in(_rk, 611), (16, 128, 128), jnp.float32))
        _g = jax.random.normal(jax.random.fold_in(_rk, 9001), (2, 1), jnp.float32)
        _g = jnp.sign(_g) * jnp.maximum(jnp.abs(_g), 1.0) + (_g == 0) * 1.0
        g_xattn = _g[0]
        g_ffn = _g[1]
        return (x, ctx_512, g_xattn, g_ffn)
    x, ctx_512, g_xattn, g_ffn = _rec_inputs()

    def _L0_xattn_setup():
        import jax, jax.numpy as jnp
        import numpy as np
        N_HEADS = 16
        N_KV_HEADS = 4
        ROPE_THETA = 10000.0
        EPS = 1e-05

        def _rms_norm(x, w):
            var = jnp.mean(x * x, axis=-1, keepdims=True)
            return x * jax.lax.rsqrt(var + EPS) * w

        def _rope_sin_cos(T, head_dim, dtype):
            inv_freq = 1.0 / ROPE_THETA ** (jnp.arange(0, head_dim, 2, dtype=jnp.float32) / head_dim)
            t = jnp.arange(T, dtype=jnp.float32)
            freqs = jnp.outer(t, inv_freq)
            emb = jnp.concatenate([freqs, freqs], -1)
            return (jnp.sin(emb).astype(dtype)[None, None], jnp.cos(emb).astype(dtype)[None, None])

        def _rotate_half(x):
            h = x.shape[-1] // 2
            x1, x2 = (x[..., :h], x[..., h:])
            return jnp.concatenate([-x2, x1], axis=-1)
        key = jax.random.key(seed)
        ks = jax.random.split(key, 6)
        B, T, C = (2, 512, 512)
        Ckv = C // N_HEADS * N_KV_HEADS
        return {'q': jax.random.normal(ks[0], (B, T, C), jnp.float32), 'k': jax.random.normal(ks[1], (B, T, Ckv), jnp.float32), 'v': jax.random.normal(ks[2], (B, T, Ckv), jnp.float32), 'q_norm_w': jnp.ones((C,), jnp.float32), 'k_norm_w': jnp.ones((Ckv,), jnp.float32), 'w_out': jax.random.normal(ks[3], (C, C), jnp.float32) * C ** (-0.5)}
    _L0_xattn_all = _L0_xattn_setup()
    _L0_xattn_in = {k: v for k, v in _L0_xattn_all.items() if k in ('q_norm_w', 'k_norm_w', 'w_out')}
    del _L0_xattn_all

    def _L0_ffn_setup():
        import jax, jax.numpy as jnp
        import numpy as np
        key = jax.random.key(seed)
        k1, k2, k3, k4, k5 = jax.random.split(key, 5)
        B, L, H, N = (2, 512, 512, 2048)
        x = jax.random.normal(k1, (B, L, H), dtype=jnp.float32)
        W0 = jax.random.normal(k2, (N, H), dtype=jnp.float32) * (1.0 / np.sqrt(H))
        bias0 = jax.random.normal(k3, (N,), dtype=jnp.float32) * 0.02
        W1 = jax.random.normal(k4, (H, N), dtype=jnp.float32) * (1.0 / np.sqrt(N))
        bias1 = jax.random.normal(k5, (H,), dtype=jnp.float32) * 0.02
        return {'x': x, 'W0': W0, 'bias0': bias0, 'W1': W1, 'bias1': bias1}
    _L0_ffn_all = _L0_ffn_setup()
    _L0_ffn_in = {k: v for k, v in _L0_ffn_all.items() if k in ('W0', 'bias0', 'W1', 'bias1')}
    del _L0_ffn_all
    return {'x': x, 'ctx_512': ctx_512, 'g_xattn': g_xattn, 'g_ffn': g_ffn, 'L0_xattn_q_norm_w': _L0_xattn_in['q_norm_w'], 'L0_xattn_k_norm_w': _L0_xattn_in['k_norm_w'], 'L0_xattn_w_out': _L0_xattn_in['w_out'], 'L0_ffn_W0': _L0_ffn_in['W0'], 'L0_ffn_bias0': _L0_ffn_in['bias0'], 'L0_ffn_W1': _L0_ffn_in['W1'], 'L0_ffn_bias1': _L0_ffn_in['bias1']}

def reference(x, ctx_512, g_xattn, g_ffn, L0_xattn_q_norm_w, L0_xattn_k_norm_w, L0_xattn_w_out, L0_ffn_W0, L0_ffn_bias0, L0_ffn_W1, L0_ffn_bias1):
    import jax
    import jax.numpy as jnp

    def _L0_xattn_ref(q, k, v, q_norm_w, k_norm_w, w_out):
        import jax, jax.numpy as jnp
        import numpy as np
        N_HEADS = 16
        N_KV_HEADS = 4
        ROPE_THETA = 10000.0
        EPS = 1e-05

        def _rms_norm(x, w):
            var = jnp.mean(x * x, axis=-1, keepdims=True)
            return x * jax.lax.rsqrt(var + EPS) * w

        def _rope_sin_cos(T, head_dim, dtype):
            inv_freq = 1.0 / ROPE_THETA ** (jnp.arange(0, head_dim, 2, dtype=jnp.float32) / head_dim)
            t = jnp.arange(T, dtype=jnp.float32)
            freqs = jnp.outer(t, inv_freq)
            emb = jnp.concatenate([freqs, freqs], -1)
            return (jnp.sin(emb).astype(dtype)[None, None], jnp.cos(emb).astype(dtype)[None, None])

        def _rotate_half(x):
            h = x.shape[-1] // 2
            x1, x2 = (x[..., :h], x[..., h:])
            return jnp.concatenate([-x2, x1], axis=-1)
        B, T, C = q.shape
        hd = C // N_HEADS
        g = N_HEADS // N_KV_HEADS
        q = _rms_norm(q, q_norm_w)
        k = _rms_norm(k, k_norm_w)
        q = q.reshape(B, T, N_HEADS, hd).transpose(0, 2, 1, 3)
        k = k.reshape(B, T, N_KV_HEADS, hd).transpose(0, 2, 1, 3)
        v = v.reshape(B, T, N_KV_HEADS, hd).transpose(0, 2, 1, 3)
        sin, cos = _rope_sin_cos(T, hd, q.dtype)
        q = q * cos + _rotate_half(q) * sin
        k = k * cos + _rotate_half(k) * sin
        qg = q.reshape(B, N_KV_HEADS, g, T, hd)
        scale = 1.0 / jnp.sqrt(jnp.asarray(hd, q.dtype))
        scores = jnp.einsum('bgnqd,bgkd->bgnqk', qg, k) * scale
        causal = jnp.tril(jnp.ones((T, T), bool))
        scores = jnp.where(causal, scores, jnp.asarray(-1e+30, scores.dtype))
        attn = jax.nn.softmax(scores, axis=-1)
        out = jnp.einsum('bgnqk,bgkd->bgnqd', attn, v)
        out = out.reshape(B, N_HEADS, T, hd).transpose(0, 2, 1, 3).reshape(B, T, C)
        return out @ w_out.T

    def _L0_ffn_ref(x, W0, bias0, W1, bias1):
        import jax, jax.numpy as jnp
        import numpy as np
        B, L, H = x.shape
        X = x.reshape(-1, H).astype(jnp.float16)
        D = jnp.dot(X.astype(jnp.float32), W0.T) + bias0
        D = jax.nn.gelu(D, approximate=False).astype(jnp.float16)
        E = jnp.dot(D.astype(jnp.float32), W1.T) + bias1
        return E.astype(jnp.float16).reshape(B, L, H)
    x = x + jnp.tanh(g_xattn[0]) * _L0_xattn_ref(_layernorm(x, axis=-1), ctx_512, ctx_512, L0_xattn_q_norm_w, L0_xattn_k_norm_w, L0_xattn_w_out)
    x = x + jnp.tanh(g_ffn[0]) * _L0_ffn_ref(_layernorm(x, axis=-1), L0_ffn_W0, L0_ffn_bias0, L0_ffn_W1, L0_ffn_bias1)
    return x

_drawn_inputs = setup_inputs


def setup_inputs(seed=0):
    import zlib

    import numpy as np

    out = dict(_drawn_inputs(seed))
    spreads = {'L0_xattn_q_norm_w': (1.0, 0.2), 'L0_xattn_k_norm_w': (1.0, 0.2)}
    factors = {'L0_ffn_bias0': 5.697, 'L0_ffn_bias1': 4.069}
    for name, (base, spread) in spreads.items():
        noise = np.random.default_rng([zlib.crc32(name.encode()), seed]).standard_normal(out[name].shape)
        drawn = base * np.exp(spread * noise) if base else spread * noise
        out[name] = jnp.asarray(drawn.astype(out[name].dtype))
    for name, factor in factors.items():
        out[name] = (out[name] * factor).astype(out[name].dtype)
    return out
```

```python
from contextlib import ExitStack

import numpy as np

import concourse.bass as bass
from concourse import mybir

P = 128
SEQS = 16
D = 512
HEADS = 16
GROUPS = 4
PER_GROUP = HEADS // GROUPS
HD = D // HEADS
KV = GROUPS * HD
QK = D + KV
HALF = HD // 2
F = 2048
KC = D // P
FC = F // P
TILES = 4
TOKENS = TILES * P
FFN_GROUPS = SEQS // TILES
EPS = 1e-5
THETA = 10000.0
MASKED = -1e30
W0_PART = 1024
W0_PARTS = KC * F // W0_PART
W1_PART = 2
W1_PARTS = FC // W1_PART

FP32 = mybir.dt.float32
FP32R = mybir.dt.float32r
FP16 = mybir.dt.float16
ALU = mybir.AluOpType
ACT = mybir.ActivationFunctionType


def build(nc, x, ctx, g_xattn, g_ffn, q_norm_w, k_norm_w, w_out_t, w0_t, bias0, w1_t, bias1, cos, sin, out):
    stack = ExitStack()
    with stack:
        def sem(name):
            return stack.enter_context(nc.semaphore(name))

        def sb(name, shape, dt=FP32, where=stack):
            return where.enter_context(nc.sbuf_tensor(name, shape, dt))

        x_all = sb("x_all", [P, SEQS, D])
        w0_hi = sb("w0_hi", [P, KC * F], FP32R)
        w0_lo = sb("w0_lo", [P, KC * F], FP32R)
        w0_raw = sb("w0_raw", [P, W0_PART])
        w1_raw = sb("w1_raw", [P, 2, W1_PART * D])
        x2_sums = sb("x2_sums", [P, SEQS, 6])
        gates = sb("gates", [P, 2])
        tanh_gates = sb("tanh_gates", [P, 2])
        minus_half = sb("minus_half", [P, SEQS])
        ident16 = sb("ident16", [P, P], FP16)

        x_landed = [sem(f"x_landed{u}") for u in range(2)]
        w0_landed = sem("w0_landed")
        w0_hi_done = sem("w0_hi_done")
        w0_split = sem("w0_split")
        w1_landed = [sem(f"w1_landed{u}") for u in range(2)]

        attention(nc, sem, x, ctx, g_xattn, g_ffn, q_norm_w, k_norm_w, w_out_t, w0_t, w1_t, cos, sin,
                  x_all, w0_hi, w0_lo, w0_raw, w1_raw, x2_sums, gates, tanh_gates, minus_half, ident16,
                  x_landed, w0_landed, w0_hi_done, w0_split, w1_landed)
        feed_forward(nc, sem, bias0, w1_t, bias1, out, x_all, w0_hi, w0_lo, w1_raw, x2_sums, tanh_gates,
                     minus_half, ident16, w1_landed)


def attention(nc, sem, x, ctx, g_xattn, g_ffn, q_norm_w, k_norm_w, w_out_t, w0_t, w1_t, cos_in, sin_in,
              x_all, w0_hi, w0_lo, w0_raw, w1_raw, x2_sums, gates, tanh_gates, minus_half, ident16,
              x_landed, w0_landed, w0_hi_done, w0_split, w1_landed):
    stack = ExitStack()
    with stack:
        def sb(name, shape, dt=FP32):
            return stack.enter_context(nc.sbuf_tensor(name, shape, dt))

        def bank(name):
            return stack.enter_context(nc.psum_tensor(name, [P, D], FP32))

        cos = sb("cos", [P, HD])
        sin = sb("sin", [P, HD])
        norm_w = sb("norm_w", [P, QK])
        rope_cos = sb("rope_cos", [P, QK])
        rope_sin = sb("rope_sin", [P, QK])
        causal = sb("causal", [P, P])
        ident = sb("ident", [P, P])
        w_out = sb("w_out", [P, PER_GROUP, D])
        ctx_all = sb("ctx_all", [P, SEQS, KV])
        x_sums = sb("x_sums", [P, 2, 6])
        k_sums = sb("k_sums", [P, 2, 6])
        x_moments = sb("x_moments", [P, 2, 2])
        k_moments = sb("k_moments", [P, 2, 2])
        k_square = sb("k_square", [P, 2, 1])
        radicand = sb("radicand", [P, 2, 2])
        rnorm = sb("rnorm", [P, 2, 2])
        qk_normed = sb("qk_normed", [P, 2, QK])
        qk_cos = sb("qk_cos", [P, QK])
        qk_sin = sb("qk_sin", [P, QK])
        qk_roped = sb("qk_roped", [P, 2, QK])
        v_tile = sb("v_tile", [P, 2, KV])
        q_t = sb("q_t", [P, 2, D])
        k_t = sb("k_t", [P, 2, P])
        probs = sb("probs", [P, 2, HEADS * P])
        minus_max = sb("minus_max", [P, 2, HEADS])
        prob_sum = sb("prob_sum", [P, 2, HEADS])
        inv_sum = sb("inv_sum", [P, D])
        probs_t = sb("probs_t", [P, GROUPS, PER_GROUP * P])
        inv_sum_t = sb("inv_sum_t", [P, D])
        mixed_t = sb("mixed_t", [P, D])
        wait_slot = sb("wait_slot", [P, 1])

        ps_scores = [bank(f"ps_scores{g}") for g in range(GROUPS)]
        ps_probs_t = [bank(f"ps_probs_t{i}") for i in range(2)]
        ps_mixed = bank("ps_mixed")
        ps_proj = bank("ps_proj")

        const_landed = sem("const_landed")
        w_out_landed = sem("w_out_landed")
        const_zeroed = sem("const_zeroed")
        const_made = sem("const_made")
        cos_made = sem("cos_made")
        rope_made = sem("rope_made")
        gates_made = sem("gates_made")
        summed = sem("summed")
        aggregated = sem("aggregated")
        squared = sem("squared")
        radicand_made = sem("radicand_made")
        rnorm_made = sem("rnorm_made")
        normed = sem("normed")
        rope_products = sem("rope_products")
        roped = sem("roped")
        v_staged = sem("v_staged")
        qk_transposed = sem("qk_transposed")
        qk_copied = sem("qk_copied")
        scored = sem("scored")
        masked = sem("masked")
        exped = sem("exped")
        inverted = sem("inverted")
        probs_transposed = sem("probs_transposed")
        probs_copied = sem("probs_copied")
        inv_transposed = sem("inv_transposed")
        inv_copied = sem("inv_copied")
        values_applied = sem("values_applied")
        divided = sem("divided")
        projected = sem("projected")
        residual_added = sem("residual_added")
        x2_summed = sem("x2_summed")

        CONSTS = 7

        class At:

            def __init__(self, b, half, u):
                self.b, self.half, self.u = b, half, u

        def at(b):
            return At(b, b // 2, b % 2)

        def seq(tensor, b):
            return tensor[:, b, :] if isinstance(b, int) else tensor[:, bass.ds(b, 1), :].rearrange("p a c -> p (a c)")

        def steps(eng, step):
            for b in range(2):
                step(at(b), at(b - 1) if b else None, at(b + 1))
            with eng.Fori(1, SEQS // 2 - 1) as i:
                step(At(2 * i, i, 0), At(2 * i - 1, i - 1, 1), At(2 * i + 1, i, 1))
                step(At(2 * i + 1, i, 1), At(2 * i, i, 0), At(2 * i + 2, i + 1, 0))
            for b in range(SEQS - 2, SEQS + 1):
                step(at(b) if b < SEQS else None, at(b - 1), at(b + 1) if b + 1 < SEQS else None)

        def after(eng, semaphore, value):
            if not (isinstance(value, int) and value <= 0):
                eng.wait_ge(semaphore, value)

        block = stack.enter_context(nc.Block())

        @block.sync
        def _(sp):
            def load(c):
                after(sp, x_landed[c.u], 32 * c.half)
                sp.dma_start(seq(x_all, c.b), x_of(c.b)).then_inc(x_landed[c.u], 16)
                sp.dma_start(seq(ctx_all, c.b), ctx_of(c.b)).then_inc(x_landed[c.u], 16)

            def x_of(b):
                return x[b, :, :] if isinstance(b, int) else x[bass.ds(b, 1), :, :].rearrange("a p c -> (a p) c")

            def ctx_of(b):
                return ctx[b, :, :] if isinstance(b, int) else ctx[bass.ds(b, 1), :, :].rearrange("a p c -> (a p) c")

            load(at(0))
            sp.dma_start(cos[:, :], cos_in).then_inc(const_landed, 16)
            sp.dma_start(sin[:, :], sin_in).then_inc(const_landed, 16)
            sp.dma_start(norm_w[:, 0:D], q_norm_w.partition_broadcast(P)).then_inc(const_landed, 16)
            sp.dma_start(norm_w[:, D:QK], k_norm_w.partition_broadcast(P)).then_inc(const_landed, 16)
            sp.dma_start(gates[:, 0:1], g_xattn.partition_broadcast(P)).then_inc(const_landed, 16)
            sp.dma_start(gates[:, 1:2], g_ffn.partition_broadcast(P)).then_inc(const_landed, 16)
            load(at(1))
            sp.dma_start(w_out[:, :, :].rearrange("p n c -> p (n c)"), w_out_t).then_inc(w_out_landed, 16)
            with sp.Fori(1, SEQS // 2) as i:
                load(At(2 * i, i, 0))
                load(At(2 * i + 1, i, 1))
            per_row = F // W0_PART
            for n in range(W0_PARTS):
                after(sp, w0_split, n)
                k, h = n // per_row, n % per_row
                sp.dma_start(w0_raw[:, :], w0_t[k * P:(k + 1) * P, h * W0_PART:(h + 1) * W0_PART])\
                    .then_inc(w0_landed, 16)
            for n in range(2):
                load_w1(sp, w1_t, w1_raw, w1_landed, n)

        @block.gpsimd
        def _(pool):
            nc.gpsimd.memset(ident[:, :], 0.0).then_inc(const_zeroed, 1)
            nc.gpsimd.memset(ident16[:, :], 0.0).then_inc(const_zeroed, 1)
            nc.gpsimd.memset(causal[:, :], 0.0).then_inc(const_zeroed, 1)
            nc.gpsimd.memset(minus_half[:, :], -0.5).then_inc(const_made, 1)
            pool.wait_ge(const_zeroed, 3)
            for m in (ident, ident16):
                nc.gpsimd.affine_select(out=m[:, :], in_=m[:, :], compare_op=ALU.not_equal, fill=1.0, base=0,
                                        pattern=[[-1, P]], channel_multiplier=1).then_inc(const_made, 1)
            nc.gpsimd.affine_select(out=causal[:, :], in_=causal[:, :], compare_op=ALU.is_ge, fill=MASKED, base=0,
                                    pattern=[[-1, P]], channel_multiplier=1).then_inc(const_made, 1)
            pool.wait_ge(const_made, 4)

            def prepare(c):
                pool.wait_ge(radicand_made, 2 * c.b + 2)
                nc.gpsimd.tensor_tensor(rnorm[:, c.u, :], radicand[:, c.u, :], minus_half[:, 0:2], ALU.pow)\
                    .then_inc(rnorm_made, 1)
                after(pool, values_applied, c.b - 1)
                nc.gpsimd.tensor_copy(v_tile[:, c.u, :], seq(ctx_all, c.b)).then_inc(v_staged, 1)
                pool.wait_ge(normed, 2 * c.b + 2)
                nc.gpsimd.tensor_tensor(qk_cos[:, :], qk_normed[:, c.u, :], rope_cos[:, :], ALU.mult)\
                    .then_inc(rope_products, 1)
                halves = qk_normed[:, c.u, :].rearrange("p (h s d) -> p h s d", s=2, d=HALF)
                table = rope_sin[:, :].rearrange("p (h s d) -> p h s d", s=2, d=HALF)
                turned = qk_sin[:, :].rearrange("p (h s d) -> p h s d", s=2, d=HALF)
                for s in range(2):
                    nc.gpsimd.tensor_tensor(turned[:, :, s, :], halves[:, :, 1 - s, :], table[:, :, s, :], ALU.mult)\
                        .then_inc(rope_products, 1)
                pool.wait_ge(rope_products, 3 * c.b + 3)
                after(pool, qk_transposed, 2 * c.b - 2)
                nc.gpsimd.tensor_tensor(qk_roped[:, c.u, :], qk_cos[:, :], qk_sin[:, :], ALU.add).then_inc(roped, 1)

            pool.wait_ge(rope_made, 3)
            prepare(at(0))
            steps(pool, lambda front, back, nxt: nxt and prepare(nxt))

        @block.scalar
        def _(act):
            act.wait_ge(const_landed, 16 * (CONSTS - 1))
            nc.scalar.activation(tanh_gates[:, :], gates[:, :], ACT.Tanh).then_inc(gates_made, 1)

            def copy_probs_t(c, g):
                act.wait_ge(probs_transposed, 4 * c.b + g + 1)
                after(act, values_applied, c.b)
                nc.scalar.activation(probs_t[:, g, :], ps_probs_t[g % 2][:, :], ACT.Copy).then_inc(probs_copied, 1)

            def step(front, back, nxt):
                if front:
                    c = front
                    act.wait_ge(qk_transposed, 2 * c.b + 1)
                    nc.scalar.activation(q_t[:, c.u, :], ps_mixed[:, :], ACT.Copy).then_inc(qk_copied, 1)
                    act.wait_ge(qk_transposed, 2 * c.b + 2)
                    nc.scalar.activation(k_t[:, c.u, :], ps_scores[0][:, 0:P], ACT.Copy).then_inc(qk_copied, 1)
                if back:
                    for g in range(GROUPS):
                        copy_probs_t(back, g)
                    act.wait_ge(inv_transposed, back.b + 1)
                    after(act, divided, back.b)
                    nc.scalar.activation(inv_sum_t[:, :], ps_proj[:, :], ACT.Copy).then_inc(inv_copied, 1)
                if front:
                    for h in range(HEADS):
                        act.wait_ge(masked, HEADS * c.b + h + 1)
                        row = probs[:, c.u, h * P:(h + 1) * P]
                        col = h % PER_GROUP * GROUPS + h // PER_GROUP
                        nc.scalar.activation(row, row, ACT.Exp, bias=minus_max[:, c.u, h:h + 1], scale=-1.0,
                                             accum_out=prob_sum[:, c.u, col:col + 1]).then_inc(exped, 1)

            steps(act, step)

        @block.vector
        def _(dve):
            dve.wait_ge(const_landed, 16 * (CONSTS - 1))
            w3 = norm_w[:, :].rearrange("p (h s d) -> p h s d", s=2, d=HALF)
            c3 = cos[:, :].rearrange("p (s d) -> p s d", s=2).unsqueeze(1)
            s3 = sin[:, :].rearrange("p (s d) -> p s d", s=2).unsqueeze(1)
            rc = rope_cos[:, :].rearrange("p (h s d) -> p h s d", s=2, d=HALF)
            rs = rope_sin[:, :].rearrange("p (h s d) -> p h s d", s=2, d=HALF)
            n = QK // HD
            nc.vector.tensor_tensor(rope_cos[:, :].rearrange("p (h e) -> p h e", e=HD),
                                    norm_w[:, :].rearrange("p (h e) -> p h e", e=HD),
                                    cos[:, :].unsqueeze(1).to_broadcast([P, n, HD]), ALU.mult).then_inc(rope_made, 1)
            for s in range(2):
                nc.vector.tensor_tensor(rs[:, :, s, :], w3[:, :, 1 - s, :],
                                        s3[:, :, s, :].to_broadcast([P, n, HALF]), ALU.mult).then_inc(rope_made, 1)

            def carry_waits():
                nc.vector.memset(wait_slot[:, :], 0.0)

            def moments(c):
                dve.wait_ge(x_landed[c.u], 32 * c.half + 32)
                nc.vector.bn_stats(x_sums[:, c.u, :], seq(x_all, c.b)).then_inc(summed, 1)
                nc.vector.bn_stats(k_sums[:, c.u, :], seq(ctx_all, c.b)).then_inc(summed, 1)
                dve.wait_ge(summed, 2 * c.b + 2)
                carry_waits()
                nc.vector.bn_aggr(x_moments[:, c.u, :], x_sums[:, c.u, :]).then_inc(aggregated, 1)
                nc.vector.bn_aggr(k_moments[:, c.u, :], k_sums[:, c.u, :]).then_inc(aggregated, 1)
                dve.wait_ge(aggregated, 2 * c.b + 2)
                mean, var = k_moments[:, c.u, 0:1], k_moments[:, c.u, 1:2]
                nc.vector.scalar_tensor_tensor(k_square[:, c.u, :], mean, mean, var, ALU.mult, ALU.add)\
                    .then_inc(squared, 1)
                nc.vector.tensor_scalar(radicand[:, c.u, 0:1], x_moments[:, c.u, 1:2], HD * (1 + EPS), HD * EPS * EPS,
                                        ALU.mult, ALU.add).then_inc(radicand_made, 1)
                dve.wait_ge(squared, c.b + 1)
                nc.vector.tensor_scalar(radicand[:, c.u, 1:2], k_square[:, c.u, :], EPS, None, ALU.add)\
                    .then_inc(radicand_made, 1)

            def normalise(c):
                dve.wait_ge(rnorm_made, c.b + 1)
                after(dve, roped, c.b - 1)
                nc.vector.tensor_scalar(qk_normed[:, c.u, 0:D].rearrange("p (n g d) -> p g n d", g=GROUPS, d=HD),
                                        seq(x_all, c.b).rearrange("p (g n d) -> p g n d", g=GROUPS, d=HD), x_moments[:, c.u, 0:1],
                                        rnorm[:, c.u, 0:1], ALU.subtract, ALU.mult).then_inc(normed, 1)
                nc.vector.tensor_scalar(qk_normed[:, c.u, D:QK], seq(ctx_all, c.b), rnorm[:, c.u, 1:2], None,
                                        ALU.mult).then_inc(normed, 1)

            def mask_and_max(c):
                dve.wait_ge(scored, c.b + 1)
                after(dve, probs_transposed, 4 * c.b - 4)
                carry_waits()
                for h in range(HEADS):
                    g, j = h // PER_GROUP, h % PER_GROUP
                    nc.vector.tensor_tensor_reduce(
                        out=probs[:, c.u, h * P:(h + 1) * P], in0=ps_scores[g][:, j * P:(j + 1) * P],
                        in1=causal[:, :], scale=-1.0, scalar=3.0e38, op0=ALU.add, op1=ALU.min,
                        accum_out=minus_max[:, c.u, h:h + 1]).then_inc(masked, 1)

            def split_w0(n):
                if isinstance(n, int):
                    hi, lo = (t[:, n * W0_PART:(n + 1) * W0_PART] for t in (w0_hi, w0_lo))
                else:
                    hi, lo = (t[:, bass.ds(n * W0_PART, W0_PART)] for t in (w0_hi, w0_lo))
                dve.wait_ge(w0_landed, 16 * n + 16)
                nc.vector.tensor_copy(hi, w0_raw[:, :]).then_inc(w0_hi_done, 1)
                dve.wait_ge(w0_hi_done, n + 1)
                nc.vector.tensor_tensor(lo, w0_raw[:, :], hi.bitcast(FP32), ALU.subtract).then_inc(w0_split, 1)

            def step(front, back, nxt):
                if back:
                    dve.wait_ge(exped, HEADS * back.b + HEADS)
                    nc.vector.reciprocal(inv_sum[:, :].rearrange("p (h d) -> p h d", d=HD),
                                         prob_sum[:, back.u, :].unsqueeze(2).to_broadcast([P, HEADS, HD]))\
                        .then_inc(inverted, 1)
                if nxt:
                    moments(nxt)
                if nxt and back and nxt.u == 0:
                    split_w0(nxt.half - 1)
                if nxt:
                    normalise(nxt)
                if back:
                    dve.wait_ge(values_applied, back.b + 1)
                    dve.wait_ge(inv_copied, back.b + 1)
                    nc.vector.tensor_tensor(mixed_t[:, :], ps_mixed[:, :], inv_sum_t[:, :], ALU.mult)\
                        .then_inc(divided, 1)
                if front:
                    mask_and_max(front)
                if back:
                    dve.wait_ge(projected, back.b + 1)
                    nc.vector.scalar_tensor_tensor(seq(x_all, back.b), ps_proj[:, :], tanh_gates[:, 0:1],
                                                   seq(x_all, back.b), ALU.mult, ALU.add).then_inc(residual_added, 1)
                    dve.wait_ge(residual_added, back.b + 1)
                    nc.vector.bn_stats(seq(x2_sums, back.b), seq(x_all, back.b)).then_inc(x2_summed, 1)

            moments(at(0))
            normalise(at(0))
            dve.wait_ge(const_made, 4)
            dve.wait_ge(gates_made, 1)
            steps(dve, step)
            split_w0(W0_PARTS - 1)

        @block.tensor
        def _(pe):
            def transpose_qk(c):
                pe.wait_ge(roped, c.b + 1)
                after(pe, divided, c.b - 1)
                for n in range(PER_GROUP):
                    last = nc.tensor.transpose(ps_mixed[:, n * P:(n + 1) * P], qk_roped[:, c.u, n * P:(n + 1) * P], ident[:, :])
                last.then_inc(qk_transposed, 1)
                after(pe, masked, HEADS * c.b)
                nc.tensor.transpose(ps_scores[0][:, 0:P], qk_roped[:, c.u, D:QK], ident[:, :])\
                    .then_inc(qk_transposed, 1)

            def scores(c):
                pe.wait_ge(qk_copied, 2 * c.b + 2)
                for n in range(PER_GROUP):
                    for g in range(GROUPS):
                        rows = slice(g * HD, (g + 1) * HD)
                        last = nc.tensor.matmul(ps_scores[g][:, n * P:(n + 1) * P], q_t[rows, c.u, n * P:(n + 1) * P],
                                                k_t[rows, c.u, :], start=True, stop=True)
                last.then_inc(scored, 1)

            def transpose_probs(c):
                for g in range(GROUPS):
                    pe.wait_ge(exped, HEADS * c.b + PER_GROUP * (g + 1))
                    after(pe, probs_copied, 4 * c.b + g - 1)
                    for n in range(PER_GROUP):
                        h = g * PER_GROUP + n
                        last = nc.tensor.transpose(ps_probs_t[g % 2][:, n * P:(n + 1) * P],
                                                   probs[:, c.u, h * P:(h + 1) * P], ident[:, :])
                    last.then_inc(probs_transposed, 1)

            def transpose_inv_sum(c):
                pe.wait_ge(inverted, c.b + 1)
                after(pe, residual_added, c.b)
                for n in range(PER_GROUP):
                    last = nc.tensor.transpose(ps_proj[:, n * P:(n + 1) * P], inv_sum[:, n * P:(n + 1) * P], ident[:, :])
                last.then_inc(inv_transposed, 1)

            def apply_values(c):
                pe.wait_ge(v_staged, c.b + 1)
                pe.wait_ge(probs_copied, 4 * c.b + 4)
                for g in range(GROUPS):
                    rows = slice(g * HD, (g + 1) * HD)
                    last = nc.tensor.matmul(ps_mixed[rows, :], v_tile[:, c.u, rows], probs_t[:, g, :],
                                            start=True, stop=True)
                last.then_inc(values_applied, 1)

            def project(c):
                pe.wait_ge(divided, c.b + 1)
                for n in range(PER_GROUP):
                    last = nc.tensor.matmul(ps_proj[:, :], mixed_t[:, n * P:(n + 1) * P], w_out[:, n, :],
                                            start=(n == 0), stop=(n == PER_GROUP - 1))
                last.then_inc(projected, 1)

            def step(front, back, nxt):
                if front:
                    transpose_qk(front)
                if back:
                    transpose_probs(back)
                if front:
                    scores(front)
                if back:
                    transpose_inv_sum(back)
                    apply_values(back)
                    project(back)

            pe.wait_ge(const_made, 4)
            pe.wait_ge(w_out_landed, 16)
            steps(pe, step)


def load_w1(sp, w1_t, w1_raw, w1_landed, n):
    view = w1_t.rearrange("(m a p) c -> m p a c", a=W1_PART, p=P)
    sp.dma_start(w1_raw[:, n % 2, :].rearrange("p (a c) -> p a c", a=W1_PART), view[n, :, :, :])\
        .then_inc(w1_landed[n % 2], 16)


def feed_forward(nc, sem, bias0_in, w1_t, bias1_in, out, x_all, w0_hi, w0_lo, w1_raw, x2_sums, tanh_gates,
                 minus_half, ident16, w1_landed):
    stack = ExitStack()
    with stack:
        def sb(name, shape, dt=FP32):
            return stack.enter_context(nc.sbuf_tensor(name, shape, dt))

        def bank(name, shape=(P, D), dt=FP32):
            return stack.enter_context(nc.psum_tensor(name, list(shape), dt))

        w1_hi = sb("w1_hi", [P, FC * D], FP32R)
        w1_lo = sb("w1_lo", [P, FC * D], FP32R)
        bias0 = sb("bias0", [P, FC])
        bias1 = sb("bias1", [P, D])
        x2_moments = sb("x2_moments", [P, SEQS, 2])
        radicand = sb("radicand2", [P, SEQS])
        rnorm = sb("rnorm2", [P, SEQS])
        x_normed = sb("x_normed", [P, TILES, D], FP16)
        x_t = sb("x_t", [P, KC, TOKENS], FP32R)
        hidden16 = sb("hidden16", [P, 2, TOKENS], FP16)
        hidden = [sb(f"hidden{i}", [P, TOKENS], FP32R) for i in range(3)]
        ffn16 = sb("ffn16", [P, TILES, D], FP16)

        ps_x_t = [bank(f"ps_x_t{i}", (P, 2, TOKENS), FP16) for i in range(2)]
        ps_hidden = [bank(f"ps_hidden{i}") for i in range(2)]
        ps_out = [bank(f"ps_out{i}") for i in range(TILES)]

        bias_landed = sem("bias_landed")
        aggregated = sem("x2_aggregated")
        radicand_made = sem("radicand2_made")
        rnorm_made = sem("rnorm2_made")
        normed = sem("x_normed_done")
        x_transposed = sem("x_transposed")
        x_copied = sem("x_copied")
        hidden_summed = sem("hidden_summed")
        hidden_rounded = sem("hidden_rounded")
        hidden_ready = sem("hidden_ready")
        hidden_used = sem("hidden_used")
        w1_hi_done = sem("w1_hi_done")
        w1_split = sem("w1_split")
        ffn_rounded = sem("ffn_rounded")
        out_ready = sem("out_ready")
        stored = sem("stored")

        def after(eng, semaphore, value):
            if not (isinstance(value, int) and value <= 0):
                eng.wait_ge(semaphore, value)

        def tile(tensor, group, t):
            if isinstance(group, int):
                return tensor[:, group * TILES + t, :]
            return tensor[:, bass.ds(group * TILES + t, 1), :].rearrange("p a c -> p (a c)")

        def column(tensor, group, t):
            if isinstance(group, int):
                return tensor[:, group * TILES + t:group * TILES + t + 1]
            return tensor[:, bass.ds(group * TILES + t, 1)]

        block = stack.enter_context(nc.Block())

        @block.sync
        def _(sp):
            sp.dma_start(bias0[:, :], bias0_in).then_inc(bias_landed, 16)
            sp.dma_start(bias1[:, :], bias1_in.partition_broadcast(P)).then_inc(bias_landed, 16)
            for n in range(2, W1_PARTS):
                sp.wait_ge(w1_split, n - 1)
                load_w1(sp, w1_t, w1_raw, w1_landed, n)
            with sp.Fori(0, FFN_GROUPS) as group:
                for t in range(TILES):
                    sp.wait_ge(out_ready, group * TILES + t + 1)
                    sp.dma_start(out[bass.ds(group * TILES + t, 1), :, :].rearrange("a p c -> (a p) c"),
                                 tile(x_all, group, t)).then_inc(stored, 16)
            sp.wait_ge(stored, 16 * SEQS)

        @block.gpsimd
        def _(pool):
            pool.wait_ge(radicand_made, 1)
            nc.gpsimd.tensor_tensor(rnorm[:, :], radicand[:, :], minus_half[:, :], ALU.pow).then_inc(rnorm_made, 1)

        @block.scalar
        def _(act):
            def activate(group, f):
                step = group * FC + f
                act.wait_ge(hidden_summed, step + 1)
                nc.scalar.activation(hidden16[:, f % 2, :], ps_hidden[f % 2][:, :], ACT.Gelu,
                                     bias=bias0[:, f:f + 1]).then_inc(hidden_rounded, 1)
                act.wait_ge(hidden_rounded, step + 1)
                after(act, hidden_used, step - 2)
                nc.scalar.activation(hidden[f % 3][:, :], hidden16[:, f % 2, :], ACT.Copy).then_inc(hidden_ready, 1)

            def copy_x_t(group):
                act.wait_ge(x_transposed, 2 * group + 2)
                after(act, hidden_summed, FC * group)
                nc.scalar.activation(x_t[:, 2:4, :], ps_x_t[1][:, :, :], ACT.Copy).then_inc(x_copied, 1)

            act.wait_ge(bias_landed, 32)
            copy_x_t(0)
            for f in range(FC):
                activate(0, f)
            with act.Fori(1, FFN_GROUPS) as group:
                copy_x_t(group)
                for f in range(FC):
                    activate(group, f)

        @block.vector
        def _(dve):
            for b in range(SEQS):
                last = nc.vector.bn_aggr(x2_moments[:, b, :], x2_sums[:, b, :])
            last.then_inc(aggregated, 1)
            dve.wait_ge(aggregated, 1)
            nc.vector.tensor_scalar(radicand[:, :], x2_moments[:, :, 1], EPS, None, ALU.add)\
                .then_inc(radicand_made, 1)

            def normalise(group):
                after(dve, x_transposed, 2 * group)
                for t in range(TILES):
                    mean = tile(x2_moments, group, t)[:, 0:1]
                    nc.vector.tensor_scalar(x_normed[:, t, :], tile(x_all, group, t), mean, column(rnorm, group, t),
                                            ALU.subtract, ALU.mult).then_inc(normed, 1)

            def copy_x_t(group):
                dve.wait_ge(x_transposed, 2 * group + 1)
                after(dve, hidden_summed, FC * group)
                nc.vector.tensor_copy(x_t[:, 0:2, :], ps_x_t[0][:, :, :]).then_inc(x_copied, 1)

            def split_w1(n):
                part = slice(n * W1_PART * D, (n + 1) * W1_PART * D)
                dve.wait_ge(w1_landed[n % 2], 16 * (n // 2) + 16)
                nc.vector.tensor_copy(w1_hi[:, part], w1_raw[:, n % 2, :]).then_inc(w1_hi_done, 1)
                dve.wait_ge(w1_hi_done, n + 1)
                nc.vector.tensor_tensor(w1_lo[:, part], w1_raw[:, n % 2, :], w1_hi[:, part].bitcast(FP32),
                                        ALU.subtract).then_inc(w1_split, 1)

            def finish(group):
                dve.wait_ge(hidden_used, FC * group + FC)
                for t in range(TILES):
                    nc.vector.tensor_tensor(ffn16[:, t, :], ps_out[t][:, :], bias1[:, :], ALU.add)\
                        .then_inc(ffn_rounded, 1)
                for t in range(TILES):
                    dve.wait_ge(ffn_rounded, TILES * group + t + 1)
                    row = tile(x_all, group, t)
                    nc.vector.scalar_tensor_tensor(row, ffn16[:, t, :], tanh_gates[:, 1:2], row, ALU.mult, ALU.add)\
                        .then_inc(out_ready, 1)
                dve.wait_ge(out_ready, TILES * group + TILES)

            dve.wait_ge(rnorm_made, 1)
            dve.wait_ge(bias_landed, 32)
            normalise(0)
            copy_x_t(0)
            for n in range(W1_PARTS):
                split_w1(n)
            with dve.Fori(0, FFN_GROUPS - 1) as group:
                normalise(group + 1)
                copy_x_t(group + 1)
                finish(group)
            finish(FFN_GROUPS - 1)

        @block.tensor
        def _(pe):
            def transpose_x(group):
                after(pe, x_copied, 2 * group)
                pe.wait_ge(normed, TILES * group + TILES)
                for k in range(KC):
                    for t in range(TILES):
                        last = nc.tensor.transpose(ps_x_t[k // 2][:, k % 2, t * P:(t + 1) * P],
                                                   x_normed[:, t, k * P:(k + 1) * P], ident16[:, :])
                    if k % 2:
                        last.then_inc(x_transposed, 1)

            def first_product(group, f):
                after(pe, hidden_rounded, group * FC + f - 1)
                for k in range(KC):
                    for half in (w0_hi, w0_lo):
                        last = nc.tensor.matmul(ps_hidden[f % 2][:, :], half[:, k * F + f * P:k * F + (f + 1) * P],
                                                x_t[:, k, :], start=(k == 0 and half is w0_hi),
                                                stop=(k == KC - 1 and half is w0_lo))
                last.then_inc(hidden_summed, 1)

            def second_product(group, f):
                pe.wait_ge(hidden_ready, group * FC + f + 1)
                pe.wait_ge(w1_split, f // W1_PART + 1)
                if f == 0:
                    after(pe, ffn_rounded, TILES * group)
                for t in range(TILES):
                    for half in (w1_hi, w1_lo):
                        last = nc.tensor.matmul(ps_out[t][:, :], hidden[f % 3][:, t * P:(t + 1) * P],
                                                half[:, f * D:(f + 1) * D], start=(f == 0 and half is w1_hi),
                                                stop=(f == FC - 1 and half is w1_lo))
                last.then_inc(hidden_used, 1)

            def products(group, transpose_next):
                pe.wait_ge(x_copied, 2 * group + 2)
                for f in range(FC):
                    first_product(group, f)
                    if f:
                        second_product(group, f - 1)
                    if f == FC // 2 and transpose_next:
                        transpose_x(group + 1)
                second_product(group, FC - 1)

            transpose_x(0)
            products(0, True)
            with pe.Fori(1, FFN_GROUPS - 1) as group:
                products(group, True)
            products(FFN_GROUPS - 1, False)


def rope_tables():
    inv_freq = np.float32(1.0) / np.float32(THETA) ** (np.arange(0, HD, 2, dtype=np.float32) / np.float32(HD))
    freqs = np.outer(np.arange(P, dtype=np.float32), inv_freq.astype(np.float32)).astype(np.float32)
    cos = np.concatenate([np.cos(freqs), np.cos(freqs)], -1).astype(np.float32)
    sin = np.concatenate([-np.sin(freqs), np.sin(freqs)], -1).astype(np.float32)
    return cos, sin


def kernel(x, ctx_512, g_xattn, g_ffn, L0_xattn_q_norm_w, L0_xattn_k_norm_w, L0_xattn_w_out, L0_ffn_W0,
           L0_ffn_bias0, L0_ffn_W1, L0_ffn_bias1):
    import concourse.bacc as bacc
    from concourse.bass_utils import run_bass_kernel_spmd

    cos, sin = rope_tables()
    w_out_t = np.asarray(L0_xattn_w_out).T.reshape(GROUPS, PER_GROUP, HD, D).transpose(0, 2, 1, 3)
    arrays = {
        "x": x, "ctx": ctx_512, "g_xattn": g_xattn, "g_ffn": g_ffn,
        "q_norm_w": np.asarray(L0_xattn_q_norm_w).reshape(GROUPS, PER_GROUP, HD).transpose(1, 0, 2).reshape(D), "k_norm_w": L0_xattn_k_norm_w,
        "w_out_t": w_out_t.reshape(P, PER_GROUP * D),
        "w0_t": np.asarray(L0_ffn_W0).T,
        "bias0": np.asarray(L0_ffn_bias0).reshape(FC, P).T,
        "w1_t": np.asarray(L0_ffn_W1).T,
        "bias1": L0_ffn_bias1, "cos": cos, "sin": sin,
    }
    arrays = {f"in_{k}": np.ascontiguousarray(v) for k, v in arrays.items()}
    nc = bacc.Bacc("TRN2", target_bir_lowering=False, num_devices=1)
    args = [nc.dram_tensor(k, v.shape, mybir.dt.from_np(v.dtype), kind="ExternalInput").ap() for k, v in arrays.items()]
    out = nc.dram_tensor("out_0", (SEQS, P, D), FP32, kind="ExternalOutput").ap()
    build(nc, *args, out)
    r = run_bass_kernel_spmd(nc, [arrays], core_ids=[0])
    return r.results[0]["out_0"]
```

```python
from contextlib import ExitStack

import numpy as np

import concourse.bass as bass
from concourse import mybir

P = 128
SEQS = 16
D = 512
HEADS = 16
GROUPS = 4
PER_GROUP = HEADS // GROUPS
HD = D // HEADS
KV = GROUPS * HD
QK = D + KV
HALF = HD // 2
F = 2048
KC = D // P
FC = F // P
TILES = 4
TOKENS = TILES * P
FFN_GROUPS = SEQS // TILES
EPS = 1e-5
THETA = 10000.0
MASKED = -1e30
W0_PART = 1024
W0_PARTS = KC * F // W0_PART
W1_PART = 2
W1_PARTS = FC // W1_PART

FP32 = mybir.dt.float32
FP32R = mybir.dt.float32r
FP16 = mybir.dt.float16
ALU = mybir.AluOpType
ACT = mybir.ActivationFunctionType


def build(nc, x, ctx, g_xattn, g_ffn, q_norm_w, k_norm_w, w_out_t, w0_t, bias0, w1_t, bias1, cos, sin, out):
    stack = ExitStack()
    with stack:
        def sem(name):
            return stack.enter_context(nc.semaphore(name))

        def sb(name, shape, dt=FP32, where=stack):
            return where.enter_context(nc.sbuf_tensor(name, shape, dt))

        x_all = sb("x_all", [P, SEQS, D])
        w0_hi = sb("w0_hi", [P, KC * F], FP32R)
        w0_lo = sb("w0_lo", [P, KC * F], FP32R)
        w0_raw = sb("w0_raw", [P, W0_PART])
        w1_raw = sb("w1_raw", [P, 2, W1_PART * D])
        x2_sums = sb("x2_sums", [P, SEQS, 6])
        gates = sb("gates", [P, 2])
        tanh_gates = sb("tanh_gates", [P, 2])
        minus_half = sb("minus_half", [P, SEQS])
        ident16 = sb("ident16", [P, P], FP16)

        x_landed = [sem(f"x_landed{u}") for u in range(2)]
        w0_landed = sem("w0_landed")
        w0_hi_done = sem("w0_hi_done")
        w0_split = sem("w0_split")
        w1_landed = [sem(f"w1_landed{u}") for u in range(2)]

        attention(nc, sem, x, ctx, g_xattn, g_ffn, q_norm_w, k_norm_w, w_out_t, w0_t, w1_t, cos, sin,
                  x_all, w0_hi, w0_lo, w0_raw, w1_raw, x2_sums, gates, tanh_gates, minus_half, ident16,
                  x_landed, w0_landed, w0_hi_done, w0_split, w1_landed)
        feed_forward(nc, sem, bias0, w1_t, bias1, out, x_all, w0_hi, w0_lo, w1_raw, x2_sums, tanh_gates,
                     minus_half, ident16, w1_landed)


def attention(nc, sem, x, ctx, g_xattn, g_ffn, q_norm_w, k_norm_w, w_out_t, w0_t, w1_t, cos_in, sin_in,
              x_all, w0_hi, w0_lo, w0_raw, w1_raw, x2_sums, gates, tanh_gates, minus_half, ident16,
              x_landed, w0_landed, w0_hi_done, w0_split, w1_landed):
    stack = ExitStack()
    with stack:
        def sb(name, shape, dt=FP32):
            return stack.enter_context(nc.sbuf_tensor(name, shape, dt))

        def bank(name):
            return stack.enter_context(nc.psum_tensor(name, [P, D], FP32))

        cos = sb("cos", [P, HD])
        sin = sb("sin", [P, HD])
        norm_w = sb("norm_w", [P, QK])
        rope_cos = sb("rope_cos", [P, QK])
        rope_sin = sb("rope_sin", [P, QK])
        causal = sb("causal", [P, P])
        ident = sb("ident", [P, P])
        w_out = sb("w_out", [P, PER_GROUP, D])
        ctx_all = sb("ctx_all", [P, SEQS, KV])
        x_sums = sb("x_sums", [P, 2, 6])
        k_sums = sb("k_sums", [P, 2, 6])
        x_moments = sb("x_moments", [P, 2, 2])
        k_moments = sb("k_moments", [P, 2, 2])
        k_square = sb("k_square", [P, 2, 1])
        radicand = sb("radicand", [P, 2, 2])
        rnorm = sb("rnorm", [P, 2, 2])
        qk_normed = sb("qk_normed", [P, 2, QK])
        qk_cos = sb("qk_cos", [P, QK])
        qk_sin = sb("qk_sin", [P, QK])
        qk_roped = sb("qk_roped", [P, 2, QK])
        v_tile = sb("v_tile", [P, 2, KV])
        q_t = sb("q_t", [P, 2, D])
        k_diag = sb("k_diag", [P, 2, GROUPS * P])
        probs = sb("probs", [P, 2, HEADS * P])
        minus_max = sb("minus_max", [P, 2, HEADS])
        prob_sum = sb("prob_sum", [P, 2, HEADS])
        inv_sum = sb("inv_sum", [P, 2, HEADS])
        inv_wide = sb("inv_wide", [P, D])
        probs_t = sb("probs_t", [P, PER_GROUP, GROUPS * P])
        inv_sum_t = sb("inv_sum_t", [P, D])
        mixed_t = sb("mixed_t", [P, D])
        wait_slots = sb("wait_slots", [P, 1 + PER_GROUP])
        ones = sb("ones", [P, D])

        ps_scores = [bank(f"ps_scores{n}") for n in range(PER_GROUP)]
        ps_probs_t = [bank(f"ps_probs_t{i}") for i in range(2)]
        ps_mixed = bank("ps_mixed")
        ps_proj = bank("ps_proj")

        const_landed = sem("const_landed")
        w_out_landed = sem("w_out_landed")
        const_zeroed = sem("const_zeroed")
        const_made = sem("const_made")
        cos_made = sem("cos_made")
        rope_made = sem("rope_made")
        gates_made = sem("gates_made")
        summed = sem("summed")
        aggregated = sem("aggregated")
        squared = sem("squared")
        radicand_made = sem("radicand_made")
        rnorm_made = sem("rnorm_made")
        normed = sem("normed")
        rope_products = sem("rope_products")
        roped = sem("roped")
        v_staged = sem("v_staged")
        qk_transposed = sem("qk_transposed")
        q_copied = sem("q_copied")
        k_copied = sem("k_copied")
        scored = sem("scored")
        masked = sem("masked")
        exped = sem("exped")
        inverted = sem("inverted")
        inv_widened = sem("inv_widened")
        k_zeroed = sem("k_zeroed")
        probs_transposed = sem("probs_transposed")
        probs_copied = [sem(f"probs_copied{u}") for u in range(2)]
        inv_transposed = sem("inv_transposed")
        inv_copied = sem("inv_copied")
        values_applied = sem("values_applied")
        divided = sem("divided")
        projected = sem("projected")
        residual_added = sem("residual_added")
        x2_summed = sem("x2_summed")

        CONSTS = 7

        class At:

            def __init__(self, b, half, u):
                self.b, self.half, self.u = b, half, u

        def at(b):
            return At(b, b // 2, b % 2) if 0 <= b < SEQS else None

        def seq(tensor, b):
            return tensor[:, b, :] if isinstance(b, int) else tensor[:, bass.ds(b, 1), :].rearrange("p a c -> p (a c)")

        def steps(eng, step):
            for b in range(2):
                step(lambda k: at(b + k))
            with eng.Fori(1, SEQS // 2 - 1) as i:
                for u in range(2):
                    step(lambda k: At(2 * i + u + k, i + (u + k) // 2, (u + k) % 2))
            for b in range(SEQS - 2, SEQS + 1):
                step(lambda k: at(b + k))

        def after(eng, semaphore, value):
            if not (isinstance(value, int) and value <= 0):
                eng.wait_ge(semaphore, value)

        block = stack.enter_context(nc.Block())

        @block.sync
        def _(sp):
            def load(c):
                after(sp, x_landed[c.u], 32 * c.half)
                sp.dma_start(seq(x_all, c.b), x_of(c.b)).then_inc(x_landed[c.u], 16)
                sp.dma_start(seq(ctx_all, c.b), ctx_of(c.b)).then_inc(x_landed[c.u], 16)

            def x_of(b):
                return x[b, :, :] if isinstance(b, int) else x[bass.ds(b, 1), :, :].rearrange("a p c -> (a p) c")

            def ctx_of(b):
                return ctx[b, :, :] if isinstance(b, int) else ctx[bass.ds(b, 1), :, :].rearrange("a p c -> (a p) c")

            load(at(0))
            sp.dma_start(cos[:, :], cos_in).then_inc(const_landed, 16)
            sp.dma_start(sin[:, :], sin_in).then_inc(const_landed, 16)
            sp.dma_start(norm_w[:, 0:D], q_norm_w.partition_broadcast(P)).then_inc(const_landed, 16)
            sp.dma_start(norm_w[:, D:QK], k_norm_w.partition_broadcast(P)).then_inc(const_landed, 16)
            sp.dma_start(gates[:, 0:1], g_xattn.partition_broadcast(P)).then_inc(const_landed, 16)
            sp.dma_start(gates[:, 1:2], g_ffn.partition_broadcast(P)).then_inc(const_landed, 16)
            load(at(1))
            sp.dma_start(w_out[:, :, :].rearrange("p n c -> p (n c)"), w_out_t).then_inc(w_out_landed, 16)
            with sp.Fori(1, SEQS // 2) as i:
                load(At(2 * i, i, 0))
                load(At(2 * i + 1, i, 1))
            per_row = F // W0_PART
            for n in range(W0_PARTS):
                after(sp, w0_split, n)
                k, h = n // per_row, n % per_row
                sp.dma_start(w0_raw[:, :], w0_t[k * P:(k + 1) * P, h * W0_PART:(h + 1) * W0_PART])\
                    .then_inc(w0_landed, 16)
            for n in range(2):
                load_w1(sp, w1_t, w1_raw, w1_landed, n)

        @block.gpsimd
        def _(pool):
            nc.gpsimd.memset(ident[:, :], 0.0).then_inc(const_zeroed, 1)
            nc.gpsimd.memset(ident16[:, :], 0.0).then_inc(const_zeroed, 1)
            nc.gpsimd.memset(causal[:, :], 0.0).then_inc(const_zeroed, 1)
            nc.gpsimd.memset(minus_half[:, :], -0.5).then_inc(const_made, 1)
            nc.gpsimd.memset(ones[:, :], 1.0).then_inc(const_made, 1)
            pool.wait_ge(const_zeroed, 3)
            for m in (ident, ident16):
                nc.gpsimd.affine_select(out=m[:, :], in_=m[:, :], compare_op=ALU.not_equal, fill=1.0, base=0,
                                        pattern=[[-1, P]], channel_multiplier=1).then_inc(const_made, 1)
            nc.gpsimd.affine_select(out=causal[:, :], in_=causal[:, :], compare_op=ALU.is_ge, fill=MASKED, base=0,
                                    pattern=[[-1, P]], channel_multiplier=1).then_inc(const_made, 1)
            pool.wait_ge(const_made, 5)

            def prepare(c):
                pool.wait_ge(radicand_made, 2 * c.b + 2)
                nc.gpsimd.tensor_tensor(rnorm[:, c.u, :], radicand[:, c.u, :], minus_half[:, 0:2], ALU.pow)\
                    .then_inc(rnorm_made, 1)
                pool.wait_ge(normed, 2 * c.b + 2)
                nc.gpsimd.tensor_tensor(qk_cos[:, :], qk_normed[:, c.u, :], rope_cos[:, :], ALU.mult)\
                    .then_inc(rope_products, 1)
                halves = qk_normed[:, c.u, :].rearrange("p (h s d) -> p h s d", s=2, d=HALF)
                table = rope_sin[:, :].rearrange("p (h s d) -> p h s d", s=2, d=HALF)
                turned = qk_sin[:, :].rearrange("p (h s d) -> p h s d", s=2, d=HALF)
                for s in range(2):
                    nc.gpsimd.tensor_tensor(turned[:, :, s, :], halves[:, :, 1 - s, :], table[:, :, s, :], ALU.mult)\
                        .then_inc(rope_products, 1)
                pool.wait_ge(rope_products, 3 * c.b + 3)
                after(pool, qk_transposed, 2 * c.b - 2)
                nc.gpsimd.tensor_tensor(qk_roped[:, c.u, :], qk_cos[:, :], qk_sin[:, :], ALU.add).then_inc(roped, 1)

            def stage_values(c):
                after(pool, values_applied, c.b - 1)
                nc.gpsimd.tensor_copy(v_tile[:, c.u, :], seq(ctx_all, c.b)).then_inc(v_staged, 1)

            def widen(c):
                pool.wait_ge(inverted, c.b + 1)
                after(pool, inv_transposed, c.b)
                nc.gpsimd.tensor_tensor(inv_wide[:, :].rearrange("p (h d) -> p h d", d=HD),
                                        inv_sum[:, c.u, :].unsqueeze(2).to_broadcast([P, HEADS, HD]),
                                        ones[:, :].rearrange("p (h d) -> p h d", d=HD), ALU.mult)\
                    .then_inc(inv_widened, 1)

            def step(s):
                back, nxt = s(-1), s(1)
                if back:
                    widen(back)
                if nxt:
                    prepare(nxt)
                    stage_values(nxt)

            pool.wait_ge(rope_made, 3)
            prepare(at(0))
            stage_values(at(0))
            steps(pool, step)

        @block.scalar
        def _(act):
            act.wait_ge(const_landed, 16 * (CONSTS - 1))
            nc.scalar.activation(tanh_gates[:, :], gates[:, :], ACT.Tanh).then_inc(gates_made, 1)

            def copy_probs_t(c, n):
                act.wait_ge(probs_transposed, PER_GROUP * c.b + n + 1)
                after(act, values_applied, c.b)
                nc.scalar.activation(probs_t[:, n, :], ps_probs_t[0][:, :], ACT.Copy).then_inc(probs_copied[0], 1)

            def step(s):
                front, back = s(0), s(-1)
                if front:
                    c = front
                    act.wait_ge(qk_transposed, 2 * c.b + 1)
                    nc.scalar.activation(q_t[:, c.u, :], ps_mixed[:, :], ACT.Copy).then_inc(q_copied, 1)
                if back:
                    copy_probs_t(back, 0)
                if front:
                    act.wait_ge(qk_transposed, 2 * c.b + 2)
                    for g in range(GROUPS):
                        rows = slice(g * HD, (g + 1) * HD)
                        nc.scalar.activation(k_diag[rows, c.u, g * P:(g + 1) * P], ps_scores[0][rows, 0:P], ACT.Copy)\
                            .then_inc(k_copied, 1)
                if back:
                    copy_probs_t(back, 2)
                    act.wait_ge(inv_transposed, back.b + 1)
                    after(act, divided, back.b)
                    nc.scalar.activation(inv_sum_t[:, :], ps_proj[:, :], ACT.Copy).then_inc(inv_copied, 1)
                if front:
                    for h in range(HEADS):
                        act.wait_ge(masked, HEADS * c.b + h + 1)
                        row = probs[:, c.u, h * P:(h + 1) * P]
                        nc.scalar.activation(row, row, ACT.Exp, bias=minus_max[:, c.u, h:h + 1], scale=-1.0,
                                             accum_out=prob_sum[:, c.u, h:h + 1]).then_inc(exped, 1)

            act.wait_ge(k_zeroed, 1)
            steps(act, step)

        @block.vector
        def _(dve):
            dve.wait_ge(const_landed, 16 * (CONSTS - 1))
            w3 = norm_w[:, :].rearrange("p (h s d) -> p h s d", s=2, d=HALF)
            c3 = cos[:, :].rearrange("p (s d) -> p s d", s=2).unsqueeze(1)
            s3 = sin[:, :].rearrange("p (s d) -> p s d", s=2).unsqueeze(1)
            rc = rope_cos[:, :].rearrange("p (h s d) -> p h s d", s=2, d=HALF)
            rs = rope_sin[:, :].rearrange("p (h s d) -> p h s d", s=2, d=HALF)
            n = QK // HD
            nc.vector.tensor_tensor(rope_cos[:, :].rearrange("p (h e) -> p h e", e=HD),
                                    norm_w[:, :].rearrange("p (h e) -> p h e", e=HD),
                                    cos[:, :].unsqueeze(1).to_broadcast([P, n, HD]), ALU.mult).then_inc(rope_made, 1)
            for s in range(2):
                nc.vector.tensor_tensor(rs[:, :, s, :], w3[:, :, 1 - s, :],
                                        s3[:, :, s, :].to_broadcast([P, n, HALF]), ALU.mult).then_inc(rope_made, 1)

            def carry_waits(slot):
                nc.vector.memset(wait_slots[:, slot:slot + 1], 0.0)

            def moments(c):
                dve.wait_ge(x_landed[c.u], 32 * c.half + 32)
                nc.vector.bn_stats(x_sums[:, c.u, :], seq(x_all, c.b)).then_inc(summed, 1)
                nc.vector.bn_stats(k_sums[:, c.u, :], seq(ctx_all, c.b)).then_inc(summed, 1)
                dve.wait_ge(summed, 2 * c.b + 2)
                carry_waits(PER_GROUP)
                nc.vector.bn_aggr(x_moments[:, c.u, :], x_sums[:, c.u, :]).then_inc(aggregated, 1)
                nc.vector.bn_aggr(k_moments[:, c.u, :], k_sums[:, c.u, :]).then_inc(aggregated, 1)
                dve.wait_ge(aggregated, 2 * c.b + 2)
                mean, var = k_moments[:, c.u, 0:1], k_moments[:, c.u, 1:2]
                nc.vector.scalar_tensor_tensor(k_square[:, c.u, :], mean, mean, var, ALU.mult, ALU.add)\
                    .then_inc(squared, 1)
                nc.vector.tensor_scalar(radicand[:, c.u, 0:1], x_moments[:, c.u, 1:2], HD * (1 + EPS), HD * EPS * EPS,
                                        ALU.mult, ALU.add).then_inc(radicand_made, 1)
                dve.wait_ge(squared, c.b + 1)
                nc.vector.tensor_scalar(radicand[:, c.u, 1:2], k_square[:, c.u, :], EPS, None, ALU.add)\
                    .then_inc(radicand_made, 1)

            def normalise(c):
                dve.wait_ge(rnorm_made, c.b + 1)
                after(dve, roped, c.b - 1)
                nc.vector.tensor_scalar(qk_normed[:, c.u, 0:D].rearrange("p (n g d) -> p g n d", g=GROUPS, d=HD),
                                        seq(x_all, c.b).rearrange("p (g n d) -> p g n d", g=GROUPS, d=HD), x_moments[:, c.u, 0:1],
                                        rnorm[:, c.u, 0:1], ALU.subtract, ALU.mult).then_inc(normed, 1)
                nc.vector.tensor_scalar(qk_normed[:, c.u, D:QK], seq(ctx_all, c.b), rnorm[:, c.u, 1:2], None,
                                        ALU.mult).then_inc(normed, 1)

            def mask_and_max(c):
                after(dve, probs_transposed, PER_GROUP * c.b - PER_GROUP)
                for n in range(PER_GROUP):
                    dve.wait_ge(scored, PER_GROUP * c.b + n + 1)
                    carry_waits(n)
                    for g in range(GROUPS):
                        h = n * GROUPS + g
                        nc.vector.tensor_tensor_reduce(
                            out=probs[:, c.u, h * P:(h + 1) * P], in0=ps_scores[n][:, g * P:(g + 1) * P],
                            in1=causal[:, :], scale=-1.0, scalar=3.0e38, op0=ALU.add, op1=ALU.min,
                            accum_out=minus_max[:, c.u, h:h + 1]).then_inc(masked, 1)

            def copy_probs_t(c, n):
                dve.wait_ge(probs_transposed, PER_GROUP * c.b + n + 1)
                after(dve, values_applied, c.b)
                nc.vector.tensor_copy(probs_t[:, n, :], ps_probs_t[1][:, :]).then_inc(probs_copied[1], 1)

            def split_w0(n):
                if isinstance(n, int):
                    hi, lo = (t[:, n * W0_PART:(n + 1) * W0_PART] for t in (w0_hi, w0_lo))
                else:
                    hi, lo = (t[:, bass.ds(n * W0_PART, W0_PART)] for t in (w0_hi, w0_lo))
                dve.wait_ge(w0_landed, 16 * n + 16)
                nc.vector.tensor_copy(hi, w0_raw[:, :]).then_inc(w0_hi_done, 1)
                dve.wait_ge(w0_hi_done, n + 1)
                nc.vector.tensor_tensor(lo, w0_raw[:, :], hi.bitcast(FP32), ALU.subtract).then_inc(w0_split, 1)

            def sum_x2(c):
                dve.wait_ge(residual_added, c.b + 1)
                nc.vector.bn_stats(seq(x2_sums, c.b), seq(x_all, c.b)).then_inc(x2_summed, 1)

            def step(s):
                front, back, nxt = s(0), s(-1), s(1)
                if back:
                    dve.wait_ge(exped, HEADS * back.b + HEADS)
                    after(dve, inv_widened, back.b - 1)
                    nc.vector.reciprocal(inv_sum[:, back.u, :], prob_sum[:, back.u, :]).then_inc(inverted, 1)
                    copy_probs_t(back, 1)
                    copy_probs_t(back, 3)
                if nxt:
                    normalise(nxt)
                if s(-2):
                    sum_x2(s(-2))
                if nxt and back and nxt.u == 0:
                    split_w0(nxt.half - 1)
                if back:
                    dve.wait_ge(values_applied, back.b + 1)
                    dve.wait_ge(inv_copied, back.b + 1)
                    nc.vector.tensor_tensor(mixed_t[:, :], ps_mixed[:, :], inv_sum_t[:, :], ALU.mult)\
                        .then_inc(divided, 1)
                if front:
                    mask_and_max(front)
                if s(2):
                    moments(s(2))
                if back:
                    dve.wait_ge(projected, back.b + 1)
                    nc.vector.scalar_tensor_tensor(seq(x_all, back.b), ps_proj[:, :], tanh_gates[:, 0:1],
                                                   seq(x_all, back.b), ALU.mult, ALU.add).then_inc(residual_added, 1)

            nc.vector.memset(k_diag[:, :, :], 0.0).then_inc(k_zeroed, 1)
            moments(at(0))
            normalise(at(0))
            moments(at(1))
            dve.wait_ge(const_made, 5)
            dve.wait_ge(gates_made, 1)
            steps(dve, step)
            sum_x2(at(SEQS - 1))
            split_w0(W0_PARTS - 1)

        @block.tensor
        def _(pe):
            def transpose_qk(c):
                pe.wait_ge(roped, c.b + 1)
                after(pe, divided, c.b - 1)
                for n in range(PER_GROUP):
                    last = nc.tensor.transpose(ps_mixed[:, n * P:(n + 1) * P], qk_roped[:, c.u, n * P:(n + 1) * P], ident[:, :])
                last.then_inc(qk_transposed, 1)
                after(pe, masked, HEADS * c.b)
                nc.tensor.transpose(ps_scores[0][:, 0:P], qk_roped[:, c.u, D:QK], ident[:, :])\
                    .then_inc(qk_transposed, 1)

            def scores(c):
                pe.wait_ge(q_copied, c.b + 1)
                pe.wait_ge(k_copied, GROUPS * (c.b + 1))
                for n in range(PER_GROUP):
                    nc.tensor.matmul(ps_scores[n][:, :], q_t[:, c.u, n * P:(n + 1) * P], k_diag[:, c.u, :],
                                     start=True, stop=True).then_inc(scored, 1)

            def transpose_probs(c):
                for n in range(PER_GROUP):
                    pe.wait_ge(exped, HEADS * c.b + GROUPS * (n + 1))
                    after(pe, probs_copied[n % 2], 2 * c.b + n // 2)
                    for g in range(GROUPS):
                        h = n * GROUPS + g
                        last = nc.tensor.transpose(ps_probs_t[n % 2][:, g * P:(g + 1) * P],
                                                   probs[:, c.u, h * P:(h + 1) * P], ident[:, :])
                    last.then_inc(probs_transposed, 1)

            def transpose_inv_sum(c):
                pe.wait_ge(inv_widened, c.b + 1)
                after(pe, residual_added, c.b)
                for n in range(PER_GROUP):
                    last = nc.tensor.transpose(ps_proj[:, n * P:(n + 1) * P], inv_wide[:, n * P:(n + 1) * P], ident[:, :])
                last.then_inc(inv_transposed, 1)

            def apply_values(c, front):
                pe.wait_ge(v_staged, c.b + 1)
                for u in range(2):
                    pe.wait_ge(probs_copied[u], 2 * c.b + 2)
                if front:
                    pe.wait_ge(q_copied, front.b + 1)
                by_group = probs_t[:, :, :].rearrange("p n (g q) -> p g n q", g=GROUPS)
                for g in range(GROUPS):
                    rows = slice(g * HD, (g + 1) * HD)
                    last = nc.tensor.matmul(ps_mixed[rows, :], v_tile[:, c.u, rows], by_group[:, g, :, :],
                                            start=True, stop=True)
                last.then_inc(values_applied, 1)

            def project(c):
                pe.wait_ge(divided, c.b + 1)
                for n in range(PER_GROUP):
                    last = nc.tensor.matmul(ps_proj[:, :], mixed_t[:, n * P:(n + 1) * P], w_out[:, n, :],
                                            start=(n == 0), stop=(n == PER_GROUP - 1))
                last.then_inc(projected, 1)

            def step(s):
                front, back = s(0), s(-1)
                if front:
                    transpose_qk(front)
                if back:
                    transpose_probs(back)
                    transpose_inv_sum(back)
                    apply_values(back, front)
                if front:
                    scores(front)
                if back:
                    project(back)

            pe.wait_ge(const_made, 5)
            pe.wait_ge(w_out_landed, 16)
            steps(pe, step)


def load_w1(sp, w1_t, w1_raw, w1_landed, n):
    view = w1_t.rearrange("(m a p) c -> m p a c", a=W1_PART, p=P)
    sp.dma_start(w1_raw[:, n % 2, :].rearrange("p (a c) -> p a c", a=W1_PART), view[n, :, :, :])\
        .then_inc(w1_landed[n % 2], 16)


def feed_forward(nc, sem, bias0_in, w1_t, bias1_in, out, x_all, w0_hi, w0_lo, w1_raw, x2_sums, tanh_gates,
                 minus_half, ident16, w1_landed):
    stack = ExitStack()
    with stack:
        def sb(name, shape, dt=FP32):
            return stack.enter_context(nc.sbuf_tensor(name, shape, dt))

        def bank(name, shape=(P, D), dt=FP32):
            return stack.enter_context(nc.psum_tensor(name, list(shape), dt))

        w1_hi = sb("w1_hi", [P, FC * D], FP32R)
        w1_lo = sb("w1_lo", [P, FC * D], FP32R)
        bias0 = sb("bias0", [P, FC])
        bias1 = sb("bias1", [P, D])
        x2_moments = sb("x2_moments", [P, SEQS, 2])
        radicand = sb("radicand2", [P, SEQS])
        rnorm = sb("rnorm2", [P, SEQS])
        x_normed = sb("x_normed", [P, TILES, D], FP16)
        x_t = sb("x_t", [P, KC, TOKENS], FP32R)
        hidden16 = sb("hidden16", [P, 2, TOKENS], FP16)
        hidden = [sb(f"hidden{i}", [P, TOKENS], FP32R) for i in range(3)]
        ffn16 = sb("ffn16", [P, TILES, D], FP16)

        ps_x_t = [bank(f"ps_x_t{i}", (P, 2, TOKENS), FP16) for i in range(2)]
        ps_hidden = [bank(f"ps_hidden{i}") for i in range(2)]
        ps_out = [bank(f"ps_out{i}") for i in range(TILES)]

        bias_landed = sem("bias_landed")
        aggregated = sem("x2_aggregated")
        radicand_made = sem("radicand2_made")
        rnorm_made = sem("rnorm2_made")
        normed = sem("x_normed_done")
        x_transposed = sem("x_transposed")
        x_copied = sem("x_copied")
        hidden_summed = sem("hidden_summed")
        hidden_rounded = sem("hidden_rounded")
        hidden_ready = sem("hidden_ready")
        hidden_used = sem("hidden_used")
        w1_hi_done = sem("w1_hi_done")
        w1_split = sem("w1_split")
        ffn_rounded = sem("ffn_rounded")
        out_ready = sem("out_ready")
        stored = sem("stored")

        def after(eng, semaphore, value):
            if not (isinstance(value, int) and value <= 0):
                eng.wait_ge(semaphore, value)

        def tile(tensor, group, t):
            if isinstance(group, int):
                return tensor[:, group * TILES + t, :]
            return tensor[:, bass.ds(group * TILES + t, 1), :].rearrange("p a c -> p (a c)")

        def column(tensor, group, t):
            if isinstance(group, int):
                return tensor[:, group * TILES + t:group * TILES + t + 1]
            return tensor[:, bass.ds(group * TILES + t, 1)]

        block = stack.enter_context(nc.Block())

        @block.sync
        def _(sp):
            sp.dma_start(bias0[:, :], bias0_in).then_inc(bias_landed, 16)
            sp.dma_start(bias1[:, :], bias1_in.partition_broadcast(P)).then_inc(bias_landed, 16)
            for n in range(2, W1_PARTS):
                sp.wait_ge(w1_split, n - 1)
                load_w1(sp, w1_t, w1_raw, w1_landed, n)
            with sp.Fori(0, FFN_GROUPS) as group:
                for t in range(TILES):
                    sp.wait_ge(out_ready, group * TILES + t + 1)
                    sp.dma_start(out[bass.ds(group * TILES + t, 1), :, :].rearrange("a p c -> (a p) c"),
                                 tile(x_all, group, t)).then_inc(stored, 16)
            sp.wait_ge(stored, 16 * SEQS)

        @block.gpsimd
        def _(pool):
            pool.wait_ge(radicand_made, 1)
            nc.gpsimd.tensor_tensor(rnorm[:, :], radicand[:, :], minus_half[:, :], ALU.pow).then_inc(rnorm_made, 1)

        @block.scalar
        def _(act):
            def activate(group, f):
                step = group * FC + f
                act.wait_ge(hidden_summed, step + 1)
                nc.scalar.activation(hidden16[:, f % 2, :], ps_hidden[f % 2][:, :], ACT.Gelu,
                                     bias=bias0[:, f:f + 1]).then_inc(hidden_rounded, 1)
                act.wait_ge(hidden_rounded, step + 1)
                after(act, hidden_used, step - 2)
                nc.scalar.activation(hidden[f % 3][:, :], hidden16[:, f % 2, :], ACT.Copy).then_inc(hidden_ready, 1)

            def copy_x_t(group):
                act.wait_ge(x_transposed, 2 * group + 2)
                after(act, hidden_summed, FC * group)
                nc.scalar.activation(x_t[:, 2:4, :], ps_x_t[1][:, :, :], ACT.Copy).then_inc(x_copied, 1)

            act.wait_ge(bias_landed, 32)
            copy_x_t(0)
            for f in range(FC):
                activate(0, f)
            with act.Fori(1, FFN_GROUPS) as group:
                copy_x_t(group)
                for f in range(FC):
                    activate(group, f)

        @block.vector
        def _(dve):
            for b in range(SEQS):
                last = nc.vector.bn_aggr(x2_moments[:, b, :], x2_sums[:, b, :])
            last.then_inc(aggregated, 1)
            dve.wait_ge(aggregated, 1)
            nc.vector.tensor_scalar(radicand[:, :], x2_moments[:, :, 1], EPS, None, ALU.add)\
                .then_inc(radicand_made, 1)

            def normalise(group):
                after(dve, x_transposed, 2 * group)
                for t in range(TILES):
                    mean = tile(x2_moments, group, t)[:, 0:1]
                    nc.vector.tensor_scalar(x_normed[:, t, :], tile(x_all, group, t), mean, column(rnorm, group, t),
                                            ALU.subtract, ALU.mult).then_inc(normed, 1)

            def copy_x_t(group):
                dve.wait_ge(x_transposed, 2 * group + 1)
                after(dve, hidden_summed, FC * group)
                nc.vector.tensor_copy(x_t[:, 0:2, :], ps_x_t[0][:, :, :]).then_inc(x_copied, 1)

            def split_w1(n):
                part = slice(n * W1_PART * D, (n + 1) * W1_PART * D)
                dve.wait_ge(w1_landed[n % 2], 16 * (n // 2) + 16)
                nc.vector.tensor_copy(w1_hi[:, part], w1_raw[:, n % 2, :]).then_inc(w1_hi_done, 1)
                dve.wait_ge(w1_hi_done, n + 1)
                nc.vector.tensor_tensor(w1_lo[:, part], w1_raw[:, n % 2, :], w1_hi[:, part].bitcast(FP32),
                                        ALU.subtract).then_inc(w1_split, 1)

            def finish(group):
                dve.wait_ge(hidden_used, FC * group + FC)
                for t in range(TILES):
                    nc.vector.tensor_tensor(ffn16[:, t, :], ps_out[t][:, :], bias1[:, :], ALU.add)\
                        .then_inc(ffn_rounded, 1)
                for t in range(TILES):
                    dve.wait_ge(ffn_rounded, TILES * group + t + 1)
                    row = tile(x_all, group, t)
                    nc.vector.scalar_tensor_tensor(row, ffn16[:, t, :], tanh_gates[:, 1:2], row, ALU.mult, ALU.add)\
                        .then_inc(out_ready, 1)
                dve.wait_ge(out_ready, TILES * group + TILES)

            dve.wait_ge(rnorm_made, 1)
            dve.wait_ge(bias_landed, 32)
            normalise(0)
            copy_x_t(0)
            for n in range(W1_PARTS):
                split_w1(n)
            with dve.Fori(0, FFN_GROUPS - 1) as group:
                normalise(group + 1)
                copy_x_t(group + 1)
                finish(group)
            finish(FFN_GROUPS - 1)

        @block.tensor
        def _(pe):
            def transpose_x(group):
                after(pe, x_copied, 2 * group)
                pe.wait_ge(normed, TILES * group + TILES)
                for k in range(KC):
                    for t in range(TILES):
                        last = nc.tensor.transpose(ps_x_t[k // 2][:, k % 2, t * P:(t + 1) * P],
                                                   x_normed[:, t, k * P:(k + 1) * P], ident16[:, :])
                    if k % 2:
                        last.then_inc(x_transposed, 1)

            def first_product(group, f):
                after(pe, hidden_rounded, group * FC + f - 1)
                for k in range(KC):
                    for half in (w0_hi, w0_lo):
                        last = nc.tensor.matmul(ps_hidden[f % 2][:, :], half[:, k * F + f * P:k * F + (f + 1) * P],
                                                x_t[:, k, :], start=(k == 0 and half is w0_hi),
                                                stop=(k == KC - 1 and half is w0_lo))
                last.then_inc(hidden_summed, 1)

            def second_product(group, f):
                pe.wait_ge(hidden_ready, group * FC + f + 1)
                pe.wait_ge(w1_split, f // W1_PART + 1)
                if f == 0:
                    after(pe, ffn_rounded, TILES * group)
                for t in range(TILES):
                    for half in (w1_hi, w1_lo):
                        last = nc.tensor.matmul(ps_out[t][:, :], hidden[f % 3][:, t * P:(t + 1) * P],
                                                half[:, f * D:(f + 1) * D], start=(f == 0 and half is w1_hi),
                                                stop=(f == FC - 1 and half is w1_lo))
                last.then_inc(hidden_used, 1)

            def products(group, transpose_next):
                pe.wait_ge(x_copied, 2 * group + 2)
                for f in range(FC):
                    first_product(group, f)
                    if f:
                        second_product(group, f - 1)
                    if f == FC // 2 and transpose_next:
                        transpose_x(group + 1)
                second_product(group, FC - 1)

            transpose_x(0)
            products(0, True)
            with pe.Fori(1, FFN_GROUPS - 1) as group:
                products(group, True)
            products(FFN_GROUPS - 1, False)


def rope_tables():
    inv_freq = np.float32(1.0) / np.float32(THETA) ** (np.arange(0, HD, 2, dtype=np.float32) / np.float32(HD))
    freqs = np.outer(np.arange(P, dtype=np.float32), inv_freq.astype(np.float32)).astype(np.float32)
    cos = np.concatenate([np.cos(freqs), np.cos(freqs)], -1).astype(np.float32)
    sin = np.concatenate([-np.sin(freqs), np.sin(freqs)], -1).astype(np.float32)
    return cos, sin


def kernel(x, ctx_512, g_xattn, g_ffn, L0_xattn_q_norm_w, L0_xattn_k_norm_w, L0_xattn_w_out, L0_ffn_W0,
           L0_ffn_bias0, L0_ffn_W1, L0_ffn_bias1):
    import concourse.bacc as bacc
    from concourse.bass_utils import run_bass_kernel_spmd

    cos, sin = rope_tables()
    w_out_t = np.asarray(L0_xattn_w_out).T.reshape(GROUPS, PER_GROUP, HD, D).transpose(0, 2, 1, 3)
    arrays = {
        "x": x, "ctx": ctx_512, "g_xattn": g_xattn, "g_ffn": g_ffn,
        "q_norm_w": np.asarray(L0_xattn_q_norm_w).reshape(GROUPS, PER_GROUP, HD).transpose(1, 0, 2).reshape(D), "k_norm_w": L0_xattn_k_norm_w,
        "w_out_t": w_out_t.reshape(P, PER_GROUP * D),
        "w0_t": np.asarray(L0_ffn_W0).T,
        "bias0": np.asarray(L0_ffn_bias0).reshape(FC, P).T,
        "w1_t": np.asarray(L0_ffn_W1).T,
        "bias1": L0_ffn_bias1, "cos": cos, "sin": sin,
    }
    arrays = {f"in_{k}": np.ascontiguousarray(v) for k, v in arrays.items()}
    nc = bacc.Bacc("TRN2", target_bir_lowering=False, num_devices=1)
    args = [nc.dram_tensor(k, v.shape, mybir.dt.from_np(v.dtype), kind="ExternalInput").ap() for k, v in arrays.items()]
    out = nc.dram_tensor("out_0", (SEQS, P, D), FP32, kind="ExternalOutput").ap()
    build(nc, *args, out)
    r = run_bass_kernel_spmd(nc, [arrays], core_ids=[0])
    return r.results[0]["out_0"]
```

```python
from contextlib import ExitStack

import numpy as np

import concourse.bass as bass
from concourse import mybir

P = 128
SEQS = 16
D = 512
HEADS = 16
GROUPS = 4
PER_GROUP = HEADS // GROUPS
HD = D // HEADS
KV = GROUPS * HD
QK = D + KV
HALF = HD // 2
F = 2048
KC = D // P
FC = F // P
TILES = 4
TOKENS = TILES * P
FFN_GROUPS = SEQS // TILES
EPS = 1e-5
THETA = 10000.0
MASKED = -1e30
W0_PART = 1024
W0_PARTS = KC * F // W0_PART
W1_PART = 2
WARM_UP = 5
W1_PARTS = FC // W1_PART

FP32 = mybir.dt.float32
FP32R = mybir.dt.float32r
FP16 = mybir.dt.float16
ALU = mybir.AluOpType
ACT = mybir.ActivationFunctionType


def build(nc, x, ctx, g_xattn, g_ffn, q_norm_w, k_norm_w, w_out_t, w0_t, bias0_in, w1_t, bias1_in, cos, sin, out):
    stack = ExitStack()
    with stack:
        def sem(name):
            return stack.enter_context(nc.semaphore(name))

        def sb(name, shape, dt=FP32):
            return stack.enter_context(nc.sbuf_tensor(name, shape, dt))

        x_all = sb("x_all", [P, SEQS, D])
        w0_hi = sb("w0_hi", [P, KC * F], FP32R)
        w0_lo = sb("w0_lo", [P, KC * F], FP32R)
        w0_raw = sb("w0_raw", [P, W0_PART])
        w1_raw = sb("w1_raw", [P, 2, W1_PART * D])
        x2_sums = sb("x2_sums", [P, SEQS, 6])
        gates = sb("gates", [P, 2])
        tanh_gates = sb("tanh_gates", [P, 2])
        minus_half = sb("minus_half", [P, SEQS])
        ident16 = sb("ident16", [P, P], FP16)

        bias0 = sb("bias0", [P, FC])
        bias1 = sb("bias1", [P, D])
        x2_moments = sb("x2_moments", [P, SEQS, 2])
        x2_radicand = sb("x2_radicand", [P, SEQS])
        x2_rnorm = sb("x2_rnorm", [P, SEQS])
        x_normed = sb("x_normed", [P, TILES, D], FP16)
        x_t = sb("x_t", [P, KC, TOKENS], FP32R)

        banks = [stack.enter_context(nc.psum_tensor(f"bank{i}", [P, D], FP32)) for i in range(8)]
        x_banks = [bank[:, :].bitcast(FP16).rearrange("p (a t) -> p a t", a=2) for bank in banks[:2]]
        ps_hidden = banks[2:4]

        x_landed = [sem(f"x_landed{u}") for u in range(2)]
        w0_landed = sem("w0_landed")
        w0_hi_done = sem("w0_hi_done")
        w0_split = sem("w0_split")
        w1_landed = [sem(f"w1_landed{u}") for u in range(2)]
        bias_landed = sem("bias_landed")
        x2_aggregated = sem("x2_aggregated")
        x2_radicand_made = sem("x2_radicand_made")
        x2_rnorm_made = sem("x2_rnorm_made")
        x_normed_made = sem("x_normed_made")
        x_transposed = sem("x_transposed")
        x_copied = sem("x_copied")
        hidden_summed = sem("hidden_summed")
        hidden_rounded = sem("hidden_rounded")


        def x2_statistics(dve, first, end):
            for b in range(first, end):
                last = nc.vector.bn_aggr(x2_moments[:, b, :], x2_sums[:, b, :])
            last.then_inc(x2_aggregated, 1)
            dve.wait_ge(x2_aggregated, 2 if first else 1)
            nc.vector.tensor_scalar(x2_radicand[:, first:end], x2_moments[:, first:end, 1], EPS, None, ALU.add)\
                .then_inc(x2_radicand_made, 1)

        def x2_inverse_root(pool, first, end):
            pool.wait_ge(x2_radicand_made, 2 if first else 1)
            nc.gpsimd.tensor_tensor(x2_rnorm[:, first:end], x2_radicand[:, first:end], minus_half[:, first:end],
                                    ALU.pow).then_inc(x2_rnorm_made, 1)

        def normalise_x2(dve, group):
            after(dve, x_transposed, 2 * group)
            for t in range(TILES):
                nc.vector.tensor_scalar(x_normed[:, t, :], tile(x_all, group, t), tile(x2_moments, group, t)[:, 0:1],
                                        column(x2_rnorm, group, t), ALU.subtract, ALU.mult).then_inc(x_normed_made, 1)

        def transpose_x(pe, group):
            after(pe, x_copied, 2 * group)
            pe.wait_ge(x_normed_made, TILES * group + TILES)
            for k in range(KC):
                for t in range(TILES):
                    last = nc.tensor.transpose(x_banks[k // 2][:, k % 2, t * P:(t + 1) * P],
                                               x_normed[:, t, k * P:(k + 1) * P], ident16[:, :])
                if k % 2:
                    last.then_inc(x_transposed, 1)

        def copy_x_t_dve(dve, group):
            dve.wait_ge(x_transposed, 2 * group + 1)
            after(dve, hidden_summed, FC * group)
            nc.vector.tensor_copy(x_t[:, 0:2, :], x_banks[0]).then_inc(x_copied, 1)

        def copy_x_t_act(act, group):
            act.wait_ge(x_transposed, 2 * group + 2)
            after(act, hidden_summed, FC * group)
            nc.scalar.activation(x_t[:, 2:4, :], x_banks[1], ACT.Copy).then_inc(x_copied, 1)

        def first_product(pe, group, f):
            after(pe, hidden_rounded, group * FC + f - 1)
            if isinstance(group, int) and group == 0 and f in (0, FC // 2):
                pe.wait_ge(w0_split, W0_PARTS if f else W0_PARTS - 1)
            for k in range(KC):
                for half in (w0_hi, w0_lo):
                    last = nc.tensor.matmul(ps_hidden[f % 2][:, :], half[:, k * F + f * P:k * F + (f + 1) * P],
                                            x_t[:, k, :], start=(k == 0 and half is w0_hi),
                                            stop=(k == KC - 1 and half is w0_lo))
            last.then_inc(hidden_summed, 1)

        attention(nc, sem, banks, x, ctx, g_xattn, g_ffn, q_norm_w, k_norm_w, w_out_t, w0_t, w1_t, cos, sin,
                  x_all, w0_hi, w0_lo, w0_raw, w1_raw, x2_sums, gates, tanh_gates, minus_half, ident16,
                  x_landed, w0_landed, w0_hi_done, w0_split, w1_landed, bias0_in, bias1_in, bias0, bias1, bias_landed,
                  x2_statistics, x2_inverse_root, normalise_x2, transpose_x, copy_x_t_dve, copy_x_t_act, first_product,
                  x2_rnorm_made, x_copied)
        feed_forward(nc, sem, banks, w1_t, out, x_all, w0_hi, w0_lo, w1_raw, tanh_gates, bias0, bias1, x_t, w1_landed,
                     bias_landed, x2_rnorm_made, x_copied, hidden_summed, hidden_rounded, x2_sums,
                     x2_statistics, x2_inverse_root, normalise_x2, transpose_x, copy_x_t_dve, copy_x_t_act,
                     first_product)


def after(eng, semaphore, value):
    if not (isinstance(value, int) and value <= 0):
        eng.wait_ge(semaphore, value)


def tile(tensor, group, t):
    if isinstance(group, int):
        return tensor[:, group * TILES + t, :]
    return tensor[:, bass.ds(group * TILES + t, 1), :].rearrange("p a c -> p (a c)")


def column(tensor, group, t):
    if isinstance(group, int):
        return tensor[:, group * TILES + t:group * TILES + t + 1]
    return tensor[:, bass.ds(group * TILES + t, 1)]


def attention(nc, sem, banks, x, ctx, g_xattn, g_ffn, q_norm_w, k_norm_w, w_out_t, w0_t, w1_t, cos_in, sin_in,
              x_all, w0_hi, w0_lo, w0_raw, w1_raw, x2_sums, gates, tanh_gates, minus_half, ident16,
              x_landed, w0_landed, w0_hi_done, w0_split, w1_landed, bias0_in, bias1_in, bias0, bias1, bias_landed,
              x2_statistics, x2_inverse_root, normalise_x2, transpose_x, copy_x_t_dve, copy_x_t_act, first_product,
              x2_rnorm_made, x_copied):
    stack = ExitStack()
    with stack:
        def sb(name, shape, dt=FP32):
            return stack.enter_context(nc.sbuf_tensor(name, shape, dt))

        cos = sb("cos", [P, HD])
        sin = sb("sin", [P, HD])
        norm_w = sb("norm_w", [P, QK])
        rope_cos = sb("rope_cos", [P, QK])
        rope_sin = sb("rope_sin", [P, QK])
        causal = sb("causal", [P, P])
        ident = sb("ident", [P, P])
        w_out = sb("w_out", [P, PER_GROUP, D])
        ctx_all = sb("ctx_all", [P, SEQS, KV])
        x_sums = sb("x_sums", [P, 2, 6])
        k_sums = sb("k_sums", [P, 2, 6])
        x_moments = sb("x_moments", [P, 2, 2])
        k_moments = sb("k_moments", [P, 2, 2])
        k_square = sb("k_square", [P, 2, 1])
        radicand = sb("radicand", [P, 2, 2])
        rnorm = sb("rnorm", [P, 2, 2])
        qk_normed = sb("qk_normed", [P, 2, QK])
        qk_cos = sb("qk_cos", [P, QK])
        qk_sin = sb("qk_sin", [P, QK])
        qk_roped = sb("qk_roped", [P, 2, QK])
        v_tile = sb("v_tile", [P, 2, KV])
        q_t = sb("q_t", [P, 2, D])
        k_diag = sb("k_diag", [P, 2, GROUPS * P])
        probs = sb("probs", [P, 2, HEADS * P])
        minus_max = sb("minus_max", [P, 2, HEADS])
        prob_sum = sb("prob_sum", [P, 2, HEADS])
        inv_sum = sb("inv_sum", [P, 2, HEADS])
        inv_wide = sb("inv_wide", [P, D])
        probs_t = sb("probs_t", [P, PER_GROUP, GROUPS * P])
        inv_sum_t = sb("inv_sum_t", [P, D])
        mixed_t = sb("mixed_t", [P, D])
        wait_slots = sb("wait_slots", [P, 1 + PER_GROUP])
        ones = sb("ones", [P, D])

        ps_scores = banks[:PER_GROUP]
        ps_mixed, ps_proj = banks[6:]
        probs_t_banks = banks[4:6] + ps_scores[2:]

        const_landed = sem("const_landed")
        gates_landed = sem("gates_landed")
        w_out_landed = sem("w_out_landed")
        const_zeroed = sem("const_zeroed")
        const_made = sem("const_made")
        cos_made = sem("cos_made")
        rope_made = sem("rope_made")
        gates_made = sem("gates_made")
        summed = sem("summed")
        aggregated = sem("aggregated")
        squared = sem("squared")
        radicand_made = sem("radicand_made")
        rnorm_made = sem("rnorm_made")
        normed = sem("normed")
        rope_products = sem("rope_products")
        roped = sem("roped")
        v_staged = sem("v_staged")
        qk_transposed = sem("qk_transposed")
        q_copied = sem("q_copied")
        k_copied = sem("k_copied")
        scored = sem("scored")
        masked = sem("masked")
        exped = sem("exped")
        inverted = sem("inverted")
        inv_widened = sem("inv_widened")
        k_zeroed = sem("k_zeroed")
        probs_transposed = sem("probs_transposed")
        probs_copied = [sem(f"probs_copied{u}") for u in range(2)]
        inv_transposed = sem("inv_transposed")
        inv_copied = sem("inv_copied")
        values_applied = sem("values_applied")
        divided = sem("divided")
        projected = sem("projected")
        residual_added = sem("residual_added")
        x2_summed = sem("x2_summed")

        class At:

            def __init__(self, b, half, u):
                self.b, self.half, self.u = b, half, u

        def at(b):
            return At(b, b // 2, b % 2) if 0 <= b < SEQS else None

        def seq(tensor, b):
            return tensor[:, b, :] if isinstance(b, int) else tensor[:, bass.ds(b, 1), :].rearrange("p a c -> p (a c)")

        def steps(eng, step):
            for b in range(2):
                step(lambda k: at(b + k))
            with eng.Fori(1, SEQS // 2 - 1) as i:
                for u in range(2):
                    step(lambda k: At(2 * i + u + k, i + (u + k) // 2, (u + k) % 2))
            for b in range(SEQS - 2, SEQS + 1):
                step(lambda k: at(b + k))

        block = stack.enter_context(nc.Block())

        @block.sync
        def _(sp):
            def load(c):
                after(sp, x_landed[c.u], 32 * c.half)
                sp.dma_start(seq(x_all, c.b), x_of(c.b)).then_inc(x_landed[c.u], 16)
                sp.dma_start(seq(ctx_all, c.b), ctx_of(c.b)).then_inc(x_landed[c.u], 16)

            def x_of(b):
                return x[b, :, :] if isinstance(b, int) else x[bass.ds(b, 1), :, :].rearrange("a p c -> (a p) c")

            def ctx_of(b):
                return ctx[b, :, :] if isinstance(b, int) else ctx[bass.ds(b, 1), :, :].rearrange("a p c -> (a p) c")

            load(at(0))
            sp.dma_start(norm_w[:, 0:D], q_norm_w.partition_broadcast(P)).then_inc(const_landed, 16)
            load(at(1))
            sp.dma_start(w_out[:, :, :].rearrange("p n c -> p (n c)"), w_out_t).then_inc(w_out_landed, 16)
            with sp.Fori(1, SEQS // 2) as i:
                load(At(2 * i, i, 0))
                load(At(2 * i + 1, i, 1))
            sp.dma_start(bias0[:, :], bias0_in).then_inc(bias_landed, 16)
            sp.dma_start(bias1[:, :], bias1_in.partition_broadcast(P)).then_inc(bias_landed, 16)
            per_row = F // W0_PART
            for n in range(W0_PARTS):
                after(sp, w0_split, n)
                k, h = n // per_row, n % per_row
                sp.dma_start(w0_raw[:, :], w0_t[k * P:(k + 1) * P, h * W0_PART:(h + 1) * W0_PART])\
                    .then_inc(w0_landed, 16)
            for n in range(2):
                load_w1(sp, w1_t, w1_raw, w1_landed, n)

        @block.gpsimd
        def _(pool):
            nc.gpsimd.memset(ident[:, :], 0.0).then_inc(const_zeroed, 1)
            nc.gpsimd.memset(ident16[:, :], 0.0).then_inc(const_zeroed, 1)
            nc.gpsimd.memset(causal[:, :], 0.0).then_inc(const_zeroed, 1)
            nc.gpsimd.memset(minus_half[:, :], -0.5).then_inc(const_made, 1)
            nc.gpsimd.memset(ones[:, :], 1.0).then_inc(const_made, 1)
            nc.gpsimd.memset(k_diag[:, :, :], 0.0).then_inc(k_zeroed, 1)
            pool.wait_ge(const_zeroed, 3)
            for m in (ident, ident16):
                nc.gpsimd.affine_select(out=m[:, :], in_=m[:, :], compare_op=ALU.not_equal, fill=1.0, base=0,
                                        pattern=[[-1, P]], channel_multiplier=1).then_inc(const_made, 1)
            nc.gpsimd.affine_select(out=causal[:, :], in_=causal[:, :], compare_op=ALU.is_ge, fill=MASKED, base=0,
                                    pattern=[[-1, P]], channel_multiplier=1).then_inc(const_made, 1)
            pool.wait_ge(const_made, 5)

            def inverse_roots(c):
                pool.wait_ge(radicand_made, 2 * c.b + 2)
                nc.gpsimd.tensor_tensor(rnorm[:, c.u, :], radicand[:, c.u, :], minus_half[:, 0:2], ALU.pow)\
                    .then_inc(rnorm_made, 1)
                pool.wait_ge(normed, 2 * c.b + 2)

            def rope_sines(c, halves_made):
                halves = qk_normed[:, c.u, :].rearrange("p (h s d) -> p h s d", s=2, d=HALF)
                table = rope_sin[:, :].rearrange("p (h s d) -> p h s d", s=2, d=HALF)
                turned = qk_sin[:, :].rearrange("p (h s d) -> p h s d", s=2, d=HALF)
                for s in halves_made:
                    nc.gpsimd.tensor_tensor(turned[:, :, s, :], halves[:, :, 1 - s, :], table[:, :, s, :], ALU.mult)\
                        .then_inc(rope_products, 1)

            def prepare(c):
                inverse_roots(c)
                pool.wait_ge(roped, c.b)
                nc.gpsimd.tensor_tensor(qk_cos[:, :], qk_normed[:, c.u, :], rope_cos[:, :], ALU.mult)\
                    .then_inc(rope_products, 1)
                rope_sines(c, (0, 1))
                pool.wait_ge(rope_products, 3 * c.b + 3)
                after(pool, qk_transposed, 2 * c.b - 2)
                nc.gpsimd.tensor_tensor(qk_roped[:, c.u, :], qk_cos[:, :], qk_sin[:, :], ALU.add).then_inc(roped, 1)

            def stage_values(c):
                after(pool, values_applied, c.b - 1)
                nc.gpsimd.tensor_copy(v_tile[:, c.u, :], seq(ctx_all, c.b)).then_inc(v_staged, 1)

            def widen(c):
                pool.wait_ge(inverted, c.b + 1)
                after(pool, inv_transposed, c.b)
                nc.gpsimd.tensor_tensor(inv_wide[:, :].rearrange("p (h d) -> p h d", d=HD),
                                        inv_sum[:, c.u, :].unsqueeze(2).to_broadcast([P, HEADS, HD]),
                                        ones[:, :].rearrange("p (h d) -> p h d", d=HD), ALU.mult)\
                    .then_inc(inv_widened, 1)

            def step(s):
                back, nxt = s(-1), s(1)
                if back:
                    widen(back)
                if nxt:
                    prepare(nxt)
                    stage_values(nxt)
                if not nxt and s(0):
                    x2_inverse_root(pool, 0, TILES)

            inverse_roots(at(0))
            pool.wait_ge(rope_made, 3)
            rope_sines(at(0), (1,))
            stage_values(at(0))
            steps(pool, step)

        @block.scalar
        def _(act):
            act.dma_start(cos[:, :], cos_in).then_inc(const_landed, 16)
            act.dma_start(sin[:, :], sin_in).then_inc(const_landed, 16)
            act.dma_start(norm_w[:, D:QK], k_norm_w.partition_broadcast(P)).then_inc(const_landed, 16)
            act.dma_start(gates[:, 0:1], g_xattn.partition_broadcast(P)).then_inc(gates_landed, 16)
            act.dma_start(gates[:, 1:2], g_ffn.partition_broadcast(P)).then_inc(gates_landed, 16)
            act.wait_ge(gates_landed, 32)
            nc.scalar.activation(tanh_gates[:, :], gates[:, :], ACT.Tanh).then_inc(gates_made, 1)

            def copy_probs_t(c, n):
                act.wait_ge(probs_transposed, PER_GROUP * c.b + n + 1)
                after(act, values_applied, c.b)
                nc.scalar.activation(probs_t[:, n, :], probs_t_banks[n][:, :], ACT.Copy).then_inc(probs_copied[0], 1)

            def exponentials(c, heads):
                for h in heads:
                    act.wait_ge(masked, HEADS * c.b + h + 1)
                    row = probs[:, c.u, h * P:(h + 1) * P]
                    nc.scalar.activation(row, row, ACT.Exp, bias=minus_max[:, c.u, h:h + 1], scale=-1.0,
                                         accum_out=prob_sum[:, c.u, h:h + 1]).then_inc(exped, 1)

            def step(s):
                front, back = s(0), s(-1)
                if front:
                    c = front
                    act.wait_ge(qk_transposed, 2 * c.b + 1)
                    nc.scalar.activation(q_t[:, c.u, :], ps_mixed[:, :], ACT.Copy).then_inc(q_copied, 1)
                    if s(-2):
                        act.wait_ge(qk_transposed, 2 * c.b + 2)
                        for g in range(GROUPS):
                            rows = slice(g * HD, (g + 1) * HD)
                            nc.scalar.activation(k_diag[rows, c.u, g * P:(g + 1) * P], ps_scores[0][rows, 0:P],
                                                 ACT.Copy).then_inc(k_copied, 1)
                if back:
                    copy_probs_t(back, 0)
                    copy_probs_t(back, 2)
                if front:
                    exponentials(front, range(PER_GROUP))
                if not front:
                    copy_x_t_act(act, 0)
                if back:
                    act.wait_ge(inv_transposed, back.b + 1)
                    after(act, divided, back.b)
                    nc.scalar.activation(inv_sum_t[:, :], ps_proj[:, :], ACT.Copy).then_inc(inv_copied, 1)
                if front:
                    exponentials(front, range(PER_GROUP, HEADS))

            act.wait_ge(k_zeroed, 1)
            steps(act, step)
            nc.scalar.activation(wait_slots[:, 0:1], tanh_gates[:, 0:1], ACT.Gelu)

        @block.vector
        def _(dve):
            def carry_waits(slot):
                nc.vector.memset(wait_slots[:, slot:slot + 1], 0.0)

            def moments(c):
                dve.wait_ge(x_landed[c.u], 32 * c.half + 32)
                nc.vector.bn_stats(x_sums[:, c.u, :], seq(x_all, c.b)).then_inc(summed, 1)
                nc.vector.bn_stats(k_sums[:, c.u, :], seq(ctx_all, c.b)).then_inc(summed, 1)
                dve.wait_ge(summed, 2 * c.b + 2)
                carry_waits(PER_GROUP)
                nc.vector.bn_aggr(x_moments[:, c.u, :], x_sums[:, c.u, :]).then_inc(aggregated, 1)
                nc.vector.bn_aggr(k_moments[:, c.u, :], k_sums[:, c.u, :]).then_inc(aggregated, 1)
                dve.wait_ge(aggregated, 2 * c.b + 2)
                mean, var = k_moments[:, c.u, 0:1], k_moments[:, c.u, 1:2]
                nc.vector.scalar_tensor_tensor(k_square[:, c.u, :], mean, mean, var, ALU.mult, ALU.add)\
                    .then_inc(squared, 1)
                nc.vector.tensor_scalar(radicand[:, c.u, 0:1], x_moments[:, c.u, 1:2], HD * (1 + EPS), HD * EPS * EPS,
                                        ALU.mult, ALU.add).then_inc(radicand_made, 1)
                dve.wait_ge(squared, c.b + 1)
                nc.vector.tensor_scalar(radicand[:, c.u, 1:2], k_square[:, c.u, :], EPS, None, ALU.add)\
                    .then_inc(radicand_made, 1)

            def normalise(c):
                dve.wait_ge(rnorm_made, c.b + 1)
                after(dve, roped, c.b - 1)
                nc.vector.tensor_scalar(qk_normed[:, c.u, 0:D].rearrange("p (n g d) -> p g n d", g=GROUPS, d=HD),
                                        seq(x_all, c.b).rearrange("p (g n d) -> p g n d", g=GROUPS, d=HD),
                                        x_moments[:, c.u, 0:1],
                                        rnorm[:, c.u, 0:1], ALU.subtract, ALU.mult).then_inc(normed, 1)
                nc.vector.tensor_scalar(qk_normed[:, c.u, D:QK], seq(ctx_all, c.b), rnorm[:, c.u, 1:2], None,
                                        ALU.mult).then_inc(normed, 1)

            def mask_and_max(c, heads):
                if 0 in heads:
                    after(dve, probs_transposed, PER_GROUP * c.b - PER_GROUP)
                for n in heads:
                    dve.wait_ge(scored, PER_GROUP * c.b + n + 1)
                    carry_waits(n)
                    for g in range(GROUPS):
                        h = n * GROUPS + g
                        nc.vector.tensor_tensor_reduce(
                            out=probs[:, c.u, h * P:(h + 1) * P], in0=ps_scores[n][:, g * P:(g + 1) * P],
                            in1=causal[:, :], scale=-1.0, scalar=3.0e38, op0=ALU.add, op1=ALU.min,
                            accum_out=minus_max[:, c.u, h:h + 1]).then_inc(masked, 1)

            def copy_probs_t(c, n):
                dve.wait_ge(probs_transposed, PER_GROUP * c.b + n + 1)
                after(dve, values_applied, c.b)
                nc.vector.tensor_copy(probs_t[:, n, :], probs_t_banks[n][:, :]).then_inc(probs_copied[1], 1)

            def split_w0(n):
                if isinstance(n, int):
                    hi, lo = (t[:, n * W0_PART:(n + 1) * W0_PART] for t in (w0_hi, w0_lo))
                else:
                    hi, lo = (t[:, bass.ds(n * W0_PART, W0_PART)] for t in (w0_hi, w0_lo))
                dve.wait_ge(w0_landed, 16 * n + 16)
                nc.vector.tensor_copy(hi, w0_raw[:, :]).then_inc(w0_hi_done, 1)
                dve.wait_ge(w0_hi_done, n + 1)
                nc.vector.tensor_tensor(lo, w0_raw[:, :], hi.bitcast(FP32), ALU.subtract).then_inc(w0_split, 1)

            def sum_x2(c):
                dve.wait_ge(residual_added, c.b + 1)
                nc.vector.bn_stats(seq(x2_sums, c.b), seq(x_all, c.b)).then_inc(x2_summed, 1)

            def copy_keys(c):
                dve.wait_ge(qk_transposed, 2 * c.b + 2)
                for g in range(GROUPS):
                    rows = slice(g * HD, (g + 1) * HD)
                    nc.vector.tensor_copy(k_diag[rows, c.u, g * P:(g + 1) * P], ps_scores[0][rows, 0:P])\
                        .then_inc(k_copied, 1)

            def step(s):
                front, back, nxt = s(0), s(-1), s(1)
                if front and not s(-2):
                    copy_keys(front)
                if back:
                    dve.wait_ge(exped, HEADS * back.b + HEADS)
                    after(dve, inv_widened, back.b - 1)
                    nc.vector.reciprocal(inv_sum[:, back.u, :], prob_sum[:, back.u, :]).then_inc(inverted, 1)
                    copy_probs_t(back, 1)
                    copy_probs_t(back, 3)
                if front and back:
                    mask_and_max(front, (0,))
                if nxt:
                    normalise(nxt)
                if front and not back:
                    mask_and_max(front, (0,))
                if not front:
                    copy_x_t_dve(dve, 0)
                if front:
                    mask_and_max(front, (1,))
                if back:
                    dve.wait_ge(values_applied, back.b + 1)
                    dve.wait_ge(inv_copied, back.b + 1)
                    nc.vector.tensor_tensor(mixed_t[:, :], ps_mixed[:, :], inv_sum_t[:, :], ALU.mult)\
                        .then_inc(divided, 1)
                if not front:
                    sum_x2(s(-2))
                if front:
                    mask_and_max(front, (2, 3))
                    if s(-2):
                        sum_x2(s(-2))
                if s(2):
                    moments(s(2))
                if front and front.u and s(-2) and nxt:
                    split_w0(front.half - 1)
                if nxt and not s(2):
                    split_w0(W0_PARTS - 2)
                if nxt and not s(2):
                    x2_statistics(dve, 0, TILES)
                if front and not nxt:
                    dve.wait_ge(x2_rnorm_made, 1)
                    normalise_x2(dve, 0)
                if not front:
                    split_w0(W0_PARTS - 1)
                if front and back:
                    dve.wait_ge(projected, back.b + 1)
                    nc.vector.scalar_tensor_tensor(seq(x_all, back.b), ps_proj[:, :], tanh_gates[:, 0:1],
                                                   seq(x_all, back.b), ALU.mult, ALU.add).then_inc(residual_added, 1)

            moments(at(0))
            dve.wait_ge(const_landed, 64)
            w3 = norm_w[:, :].rearrange("p (h s d) -> p h s d", s=2, d=HALF)
            s3 = sin[:, :].rearrange("p (s d) -> p s d", s=2).unsqueeze(1)
            rs = rope_sin[:, :].rearrange("p (h s d) -> p h s d", s=2, d=HALF)
            n = QK // HD
            nc.vector.tensor_tensor(rope_cos[:, :].rearrange("p (h e) -> p h e", e=HD),
                                    norm_w[:, :].rearrange("p (h e) -> p h e", e=HD),
                                    cos[:, :].unsqueeze(1).to_broadcast([P, n, HD]), ALU.mult).then_inc(rope_made, 1)
            for s in range(2):
                nc.vector.tensor_tensor(rs[:, :, s, :], w3[:, :, 1 - s, :],
                                        s3[:, :, s, :].to_broadcast([P, n, HALF]), ALU.mult).then_inc(rope_made, 1)
            normalise(at(0))
            dve.wait_ge(normed, 2)
            dve.wait_ge(rope_made, 3)
            nc.vector.tensor_tensor(qk_cos[:, :], qk_normed[:, 0, :], rope_cos[:, :], ALU.mult)\
                .then_inc(rope_products, 1)
            nc.vector.tensor_tensor(qk_sin[:, :].rearrange("p (h s d) -> p h s d", s=2, d=HALF)[:, :, 0, :],
                                    qk_normed[:, 0, :].rearrange("p (h s d) -> p h s d", s=2, d=HALF)[:, :, 1, :],
                                    rs[:, :, 0, :], ALU.mult).then_inc(rope_products, 1)
            dve.wait_ge(rope_products, 3)
            nc.vector.tensor_tensor(qk_roped[:, 0, :], qk_cos[:, :], qk_sin[:, :], ALU.add).then_inc(roped, 1)
            moments(at(1))
            dve.wait_ge(const_made, 5)
            dve.wait_ge(k_zeroed, 1)
            dve.wait_ge(gates_made, 1)
            steps(dve, step)

        @block.tensor
        def _(pe):
            def transpose_qk(c):
                pe.wait_ge(roped, c.b + 1)
                after(pe, divided, c.b - 1)
                for n in range(PER_GROUP):
                    cols = slice(n * P, (n + 1) * P)
                    last = nc.tensor.transpose(ps_mixed[:, cols], qk_roped[:, c.u, cols], ident[:, :])
                last.then_inc(qk_transposed, 1)
                after(pe, masked, HEADS * c.b)
                nc.tensor.transpose(ps_scores[0][:, 0:P], qk_roped[:, c.u, D:QK], ident[:, :])\
                    .then_inc(qk_transposed, 1)

            def scores(c, heads):
                if 0 in heads:
                    pe.wait_ge(q_copied, c.b + 1)
                    pe.wait_ge(k_copied, GROUPS * (c.b + 1))
                for n in heads:
                    nc.tensor.matmul(ps_scores[n][:, :], q_t[:, c.u, n * P:(n + 1) * P], k_diag[:, c.u, :],
                                     start=True, stop=True).then_inc(scored, 1)

            def transpose_probs(c):
                for n in range(PER_GROUP):
                    pe.wait_ge(exped, HEADS * c.b + GROUPS * (n + 1))
                    if n < 2:
                        after(pe, probs_copied[n], 2 * c.b)
                    for g in range(GROUPS):
                        h = n * GROUPS + g
                        last = nc.tensor.transpose(probs_t_banks[n][:, g * P:(g + 1) * P],
                                                   probs[:, c.u, h * P:(h + 1) * P], ident[:, :])
                    last.then_inc(probs_transposed, 1)

            def transpose_inv_sum(c):
                pe.wait_ge(inv_widened, c.b + 1)
                after(pe, residual_added, c.b)
                for n in range(PER_GROUP):
                    cols = slice(n * P, (n + 1) * P)
                    last = nc.tensor.transpose(ps_proj[:, cols], inv_wide[:, cols], ident[:, :])
                last.then_inc(inv_transposed, 1)

            def apply_values(c, front):
                pe.wait_ge(v_staged, c.b + 1)
                for u in range(2):
                    pe.wait_ge(probs_copied[u], 2 * c.b + 2)
                if front:
                    pe.wait_ge(q_copied, front.b + 1)
                by_group = probs_t[:, :, :].rearrange("p n (g q) -> p g n q", g=GROUPS)
                for g in range(GROUPS):
                    rows = slice(g * HD, (g + 1) * HD)
                    last = nc.tensor.matmul(ps_mixed[rows, :], v_tile[:, c.u, rows], by_group[:, g, :, :],
                                            start=True, stop=True)
                last.then_inc(values_applied, 1)

            def project(c):
                pe.wait_ge(divided, c.b + 1)
                for n in range(PER_GROUP):
                    last = nc.tensor.matmul(ps_proj[:, :], mixed_t[:, n * P:(n + 1) * P], w_out[:, n, :],
                                            start=(n == 0), stop=(n == PER_GROUP - 1))
                last.then_inc(projected, 1)

            def step(s):
                front, back = s(0), s(-1)
                if front:
                    transpose_qk(front)
                if back:
                    transpose_probs(back)
                if front:
                    scores(front, (0, 1))
                else:
                    transpose_x(pe, 0)
                if back:
                    transpose_inv_sum(back)
                    apply_values(back, front)
                if front:
                    scores(front, (2, 3))
                else:
                    pe.wait_ge(x_copied, 2)
                    first_product(pe, 0, 0)
                if back:
                    project(back)

            pe.wait_ge(k_zeroed, 1)
            for _ in range(WARM_UP):
                nc.tensor.matmul(ps_proj[:, :], k_diag[:, 0, 0:P], k_diag[:, 1, :], start=True, stop=True)
            pe.wait_ge(const_made, 5)
            pe.wait_ge(w_out_landed, 16)
            steps(pe, step)


def load_w1(sp, w1_t, w1_raw, w1_landed, n):
    view = w1_t.rearrange("(m a p) c -> m p a c", a=W1_PART, p=P)
    sp.dma_start(w1_raw[:, n % 2, :].rearrange("p (a c) -> p a c", a=W1_PART), view[n, :, :, :])\
        .then_inc(w1_landed[n % 2], 16)


def feed_forward(nc, sem, banks, w1_t, out, x_all, w0_hi, w0_lo, w1_raw, tanh_gates, bias0, bias1, x_t, w1_landed,
                 bias_landed, x2_rnorm_made, x_copied, hidden_summed, hidden_rounded, x2_sums,
                 x2_statistics, x2_inverse_root, normalise_x2, transpose_x, copy_x_t_dve, copy_x_t_act, first_product):
    stack = ExitStack()
    with stack:
        def sb(name, shape, dt=FP32):
            return stack.enter_context(nc.sbuf_tensor(name, shape, dt))

        w1_hi = sb("w1_hi", [P, FC * D], FP32R)
        w1_lo = sb("w1_lo", [P, FC * D], FP32R)
        hidden16 = sb("hidden16", [P, 2, TOKENS], FP16)
        hidden = [sb(f"hidden{i}", [P, TOKENS], FP32R) for i in range(3)]
        ffn16 = sb("ffn16", [P, TILES, D], FP16)
        ffn_gated = sb("ffn_gated", [P, 2, D])

        ps_hidden, ps_out = banks[2:4], banks[4:]

        hidden_ready = sem("hidden_ready")
        hidden_used = sem("hidden_used")
        w1_hi_done = sem("w1_hi_done")
        last_residual_added = sem("last_residual_added")
        last_summed = sem("last_summed")
        w1_split = sem("w1_split")
        tile_summed = sem("tile_summed")
        ffn_rounded = sem("ffn_rounded")
        out_ready = sem("out_ready")
        gated = sem("gated")
        pool_out_ready = sem("pool_out_ready")
        stored = sem("stored")

        block = stack.enter_context(nc.Block())

        @block.sync
        def _(sp):
            for n in range(2, W1_PARTS):
                sp.wait_ge(w1_split, n - 1)
                load_w1(sp, w1_t, w1_raw, w1_landed, n)
            with sp.Fori(0, FFN_GROUPS - 1) as group:
                for t in range(TILES):
                    sp.wait_ge(out_ready, group * TILES + t + 1)
                    sp.dma_start(out[bass.ds(group * TILES + t, 1), :, :].rearrange("a p c -> (a p) c"),
                                 tile(x_all, group, t)).then_inc(stored, 16)
            group = FFN_GROUPS - 1
            for t in (0, 2, 1, 3):
                if t < 2:
                    sp.wait_ge(pool_out_ready, t + 1)
                else:
                    sp.wait_ge(out_ready, group * TILES + t - 1)
                sp.dma_start(out[group * TILES + t, :, :], tile(x_all, group, t)).then_inc(stored, 16)
            sp.wait_ge(stored, 16 * SEQS)

        @block.gpsimd
        def _(pool):
            x2_inverse_root(pool, TILES, SEQS)
            for t in range(2):
                pool.wait_ge(gated, t + 1)
                row = tile(x_all, FFN_GROUPS - 1, t)
                nc.gpsimd.tensor_tensor(row, ffn_gated[:, t, :], row, ALU.add).then_inc(pool_out_ready, 1)

        @block.scalar
        def _(act):
            def activate(group, f):
                step = group * FC + f
                act.wait_ge(hidden_summed, step + 1)
                nc.scalar.activation(hidden16[:, f % 2, :], ps_hidden[f % 2][:, :], ACT.Gelu,
                                     bias=bias0[:, f:f + 1]).then_inc(hidden_rounded, 1)
                act.wait_ge(hidden_rounded, step + 1)
                if f >= 3:
                    act.wait_ge(hidden_used, (FC - 1) * group + f - 2)
                else:
                    after(act, tile_summed, TILES * group)
                nc.scalar.activation(hidden[f % 3][:, :], hidden16[:, f % 2, :], ACT.Copy).then_inc(hidden_ready, 1)

            act.wait_ge(bias_landed, 32)
            for f in range(FC):
                activate(0, f)
            with act.Fori(1, FFN_GROUPS) as group:
                copy_x_t_act(act, group)
                for f in range(FC):
                    activate(group, f)
            for t in range(2):
                act.wait_ge(ffn_rounded, TILES * (FFN_GROUPS - 1) + t + 1)
                nc.scalar.activation(ffn_gated[:, t, :], ffn16[:, t, :], ACT.Copy, scale=tanh_gates[:, 1:2])\
                    .then_inc(gated, 1)

        @block.vector
        def _(dve):
            def split_w1(n):
                part = slice(n * W1_PART * D, (n + 1) * W1_PART * D)
                dve.wait_ge(w1_landed[n % 2], 16 * (n // 2) + 16)
                nc.vector.tensor_copy(w1_hi[:, part], w1_raw[:, n % 2, :]).then_inc(w1_hi_done, 1)
                dve.wait_ge(w1_hi_done, n + 1)
                nc.vector.tensor_tensor(w1_lo[:, part], w1_raw[:, n % 2, :], w1_hi[:, part].bitcast(FP32),
                                        ALU.subtract).then_inc(w1_split, 1)

            def round_tile(group, t):
                dve.wait_ge(tile_summed, TILES * group + t + 1)
                nc.vector.tensor_tensor(ffn16[:, t, :], ps_out[t][:, :], bias1[:, :], ALU.add).then_inc(ffn_rounded, 1)

            def add_residual(group, t):
                dve.wait_ge(ffn_rounded, TILES * group + t + 1)
                row = tile(x_all, group, t)
                nc.vector.scalar_tensor_tensor(row, ffn16[:, t, :], tanh_gates[:, 1:2], row, ALU.mult, ALU.add)\
                    .then_inc(out_ready, 1)

            def finish(group):
                for t in range(TILES):
                    round_tile(group, t)
                for t in range(TILES):
                    add_residual(group, t)
                dve.wait_ge(out_ready, TILES * group + TILES)

            def last_finish(group):
                for t in range(TILES):
                    round_tile(group, t)
                    if t >= 2:
                        add_residual(group, t)

            split_w1(0)
            last_tile = x_all[:, SEQS - 1, :]
            nc.vector.scalar_tensor_tensor(last_tile, ps_out[TILES - 1][:, :], tanh_gates[:, 0:1], last_tile,
                                           ALU.mult, ALU.add).then_inc(last_residual_added, 1)
            dve.wait_ge(last_residual_added, 1)
            nc.vector.bn_stats(x2_sums[:, SEQS - 1, :], last_tile).then_inc(last_summed, 1)
            split_w1(1)
            dve.wait_ge(last_summed, 1)
            x2_statistics(dve, TILES, SEQS)
            for n in range(2, W1_PARTS):
                split_w1(n)
            dve.wait_ge(x2_rnorm_made, 2)
            dve.wait_ge(bias_landed, 32)
            with dve.Fori(0, FFN_GROUPS - 1) as group:
                normalise_x2(dve, group + 1)
                copy_x_t_dve(dve, group + 1)
                finish(group)
            last_finish(FFN_GROUPS - 1)

        @block.tensor
        def _(pe):
            def second_product(group, f, t, last_of_block):
                if f == 0 and t == 0:
                    after(pe, ffn_rounded, TILES * group)
                if f == 0 and t == TILES - 1 and isinstance(group, int) and group == 0:
                    pe.wait_ge(last_residual_added, 1)
                for half in (w1_hi, w1_lo):
                    last = nc.tensor.matmul(ps_out[t][:, :], hidden[f % 3][:, t * P:(t + 1) * P],
                                            half[:, f * D:(f + 1) * D], start=(f == 0 and half is w1_hi),
                                            stop=(f == FC - 1 and half is w1_lo))
                if f == FC - 1:
                    last.then_inc(tile_summed, 1)
                elif last_of_block:
                    last.then_inc(hidden_used, 1)

            def second_products(group, f):
                pe.wait_ge(hidden_ready, group * FC + f + 1)
                pe.wait_ge(w1_split, f // W1_PART + 1)
                for t in range(TILES):
                    second_product(group, f, t, t == TILES - 1)

            def products(group):
                pe.wait_ge(x_copied, 2 * group + 2)
                for f in range(FC):
                    if f or not isinstance(group, int):
                        first_product(pe, group, f)
                    if f:
                        second_products(group, f - 1)
                    if f == FC // 2:
                        transpose_x(pe, group + 1)
                second_products(group, FC - 1)

            def last_products(group):
                pe.wait_ge(x_copied, 2 * group + 2)
                for f in range(FC):
                    first_product(pe, group, f)
                    if 0 < f < FC - 2:
                        second_products(group, f - 1)
                second_products(group, FC - 3)
                for t in range(TILES):
                    for f in range(FC - 2, FC):
                        if t == 0:
                            pe.wait_ge(hidden_ready, group * FC + f + 1)
                        second_product(group, f, t, t == TILES - 1)

            products(0)
            with pe.Fori(1, FFN_GROUPS - 1) as group:
                products(group)
            last_products(FFN_GROUPS - 1)


def rope_tables():
    inv_freq = np.float32(1.0) / np.float32(THETA) ** (np.arange(0, HD, 2, dtype=np.float32) / np.float32(HD))
    freqs = np.outer(np.arange(P, dtype=np.float32), inv_freq.astype(np.float32)).astype(np.float32)
    cos = np.concatenate([np.cos(freqs), np.cos(freqs)], -1).astype(np.float32)
    sin = np.concatenate([-np.sin(freqs), np.sin(freqs)], -1).astype(np.float32)
    return cos, sin


def kernel(x, ctx_512, g_xattn, g_ffn, L0_xattn_q_norm_w, L0_xattn_k_norm_w, L0_xattn_w_out, L0_ffn_W0,
           L0_ffn_bias0, L0_ffn_W1, L0_ffn_bias1):
    import concourse.bacc as bacc
    from concourse.bass_utils import run_bass_kernel_spmd

    cos, sin = rope_tables()
    w_out_t = np.asarray(L0_xattn_w_out).T.reshape(GROUPS, PER_GROUP, HD, D).transpose(0, 2, 1, 3)
    q_norm_w = np.asarray(L0_xattn_q_norm_w).reshape(GROUPS, PER_GROUP, HD).transpose(1, 0, 2)
    arrays = {
        "x": x, "ctx": ctx_512, "g_xattn": g_xattn, "g_ffn": g_ffn,
        "q_norm_w": q_norm_w.reshape(D), "k_norm_w": L0_xattn_k_norm_w,
        "w_out_t": w_out_t.reshape(P, PER_GROUP * D),
        "w0_t": np.asarray(L0_ffn_W0).T,
        "bias0": np.asarray(L0_ffn_bias0).reshape(FC, P).T,
        "w1_t": np.asarray(L0_ffn_W1).T,
        "bias1": L0_ffn_bias1, "cos": cos, "sin": sin,
    }
    arrays = {f"in_{k}": np.ascontiguousarray(v) for k, v in arrays.items()}
    nc = bacc.Bacc("TRN2", target_bir_lowering=False, num_devices=1)
    args = [nc.dram_tensor(k, v.shape, mybir.dt.from_np(v.dtype), kind="ExternalInput").ap() for k, v in arrays.items()]
    out = nc.dram_tensor("out_0", (SEQS, P, D), FP32, kind="ExternalOutput").ap()
    build(nc, *args, out)
    r = run_bass_kernel_spmd(nc, [arrays], core_ids=[0])
    return r.results[0]["out_0"]
```
